# Optimizing a Trainium2 kernel written in Bass

```python
import numpy as np
import jax
import jax.numpy as jnp

def _softmax(x, axis=-1):
    return jax.nn.softmax(x, axis=axis)

def _gelu(x):
    return jax.nn.gelu(x, approximate=True)

def _silu(x):
    return jax.nn.silu(x)

def _sigmoid(x):
    return jax.nn.sigmoid(x)

def _layernorm(x, axis=-1, eps=1e-05):
    m = jnp.mean(x, axis=axis, keepdims=True)
    v = jnp.var(x, axis=axis, keepdims=True)
    return (x - m) / jnp.sqrt(v + eps)

def _scatter_add(tgt, idx, src, axis=0):
    return tgt.at[idx].add(src)

def _segment_sum(src, seg, n):
    return jax.ops.segment_sum(src, seg, n)
kernel_name = 'mk_adj_preln_d1_adj_r2_95023a'

def setup_inputs(seed: int=0):
    np.random.seed(seed)
    _w = jnp.asarray

    def _rec_inputs():
        import jax
        import jax.numpy as jnp
        _gk = jax.random.key(seed)
        x = -1.394e-06 + 0.9999 * jax.random.normal(jax.random.fold_in(_gk, 1), (4096, 256), jnp.float32)
        _a = jax.random.bernoulli(jax.random.fold_in(_gk, 2), 0.000976562, (4096, 4096))
        _a = jnp.logical_or(_a, jnp.swapaxes(_a, -1, -2))
        _a = jnp.logical_or(_a, jnp.eye(4096, dtype=bool))
        adj = _a
        return (x, adj)
    x, adj = _rec_inputs()

    def _L0_gnn_setup():
        import jax, jax.numpy as jnp
        import numpy as np
        import math
        N = 4096
        D_IN = 256
        LOCAL_D = 256
        GLOBAL_D = 256
        key = jax.random.key(seed)
        ks = jax.random.split(key, 16)
        s = 1.0 / math.sqrt(D_IN)
        adj = jax.random.bernoulli(ks[0], 0.01, (N, N))
        adj = adj | jnp.eye(N, dtype=bool)
        return {'adj_matrix': adj, 'x': jax.random.normal(ks[1], (N, D_IN), jnp.float32), 'masked_x': jax.random.normal(ks[2], (N, D_IN), jnp.float32), 'Wlq': jax.random.normal(ks[3], (D_IN, LOCAL_D), jnp.float32) * s, 'Wlk': jax.random.normal(ks[4], (D_IN, LOCAL_D), jnp.float32) * s, 'Wlv': jax.random.normal(ks[5], (D_IN, D_IN), jnp.float32) * s, 'blv': jax.random.normal(ks[6], (D_IN,), jnp.float32) * 0.01, 'Wgq': jax.random.normal(ks[7], (D_IN, GLOBAL_D), jnp.float32) * s, 'Wgk': jax.random.normal(ks[8], (D_IN, GLOBAL_D), jnp.float32) * s, 'Wgv': jax.random.normal(ks[9], (D_IN, D_IN), jnp.float32) * s, 'bgv': jax.random.normal(ks[10], (D_IN,), jnp.float32) * 0.01, 'Wes': jax.random.normal(ks[11], (D_IN, 1), jnp.float32) * s, 'Wev': jax.random.normal(ks[12], (D_IN, D_IN), jnp.float32) * s, 'bev': jax.random.normal(ks[13], (D_IN,), jnp.float32) * 0.01}
    _L0_gnn_all = _L0_gnn_setup()
    _L0_gnn_in = {k: v for k, v in _L0_gnn_all.items() if k in ('masked_x', 'Wlq', 'Wlk', 'Wlv', 'blv', 'Wgq', 'Wgk', 'Wgv', 'bgv', 'Wes', 'Wev', 'bev')}
    del _L0_gnn_all
    return {'x': x, 'adj': adj, 'L0_gnn_masked_x': _L0_gnn_in['masked_x'], 'L0_gnn_Wlq': _L0_gnn_in['Wlq'], 'L0_gnn_Wlk': _L0_gnn_in['Wlk'], 'L0_gnn_Wlv': _L0_gnn_in['Wlv'], 'L0_gnn_blv': _L0_gnn_in['blv'], 'L0_gnn_Wgq': _L0_gnn_in['Wgq'], 'L0_gnn_Wgk': _L0_gnn_in['Wgk'], 'L0_gnn_Wgv': _L0_gnn_in['Wgv'], 'L0_gnn_bgv': _L0_gnn_in['bgv'], 'L0_gnn_Wes': _L0_gnn_in['Wes'], 'L0_gnn_Wev': _L0_gnn_in['Wev'], 'L0_gnn_bev': _L0_gnn_in['bev']}

def reference(x, adj, L0_gnn_masked_x, L0_gnn_Wlq, L0_gnn_Wlk, L0_gnn_Wlv, L0_gnn_blv, L0_gnn_Wgq, L0_gnn_Wgk, L0_gnn_Wgv, L0_gnn_bgv, L0_gnn_Wes, L0_gnn_Wev, L0_gnn_bev):
    import jax
    import jax.numpy as jnp

    def _L0_gnn_ref(adj_matrix, x, masked_x, Wlq, Wlk, Wlv, blv, Wgq, Wgk, Wgv, bgv, Wes, Wev, bev):
        import jax, jax.numpy as jnp
        import numpy as np
        import math
        N = 4096
        D_IN = 256
        LOCAL_D = 256
        GLOBAL_D = 256
        scale = 1.0 / math.sqrt(D_IN)
        x_bar = jnp.mean(x, axis=0, keepdims=True)
        lQ = masked_x @ Wlq
        lK = x @ Wlk
        lV = x @ Wlv + blv
        gQ = masked_x @ Wgq
        gK = x_bar @ Wgk
        gV = x_bar @ Wgv + bgv
        es = masked_x @ Wes
        eV = masked_x @ Wev + bev
        local_scores = lQ @ lK.T * scale
        local_scores = jnp.where(adj_matrix, local_scores, jnp.float32(-1000000000.0))
        global_scores = gQ @ gK.T * scale
        max_score = jnp.maximum(jnp.max(local_scores, axis=1, keepdims=True), jnp.maximum(global_scores, es))
        le = jnp.exp(local_scores - max_score)
        ge = jnp.exp(global_scores - max_score)
        ee = jnp.exp(es - max_score)
        denom = jnp.sum(le, axis=-1, keepdims=True) + ge + ee
        res = le / denom @ lV + ge / denom * gV + ee / denom * eV
        x_recon = jnp.maximum(res, masked_x)
        return x_recon
    h = jnp.maximum(_layernorm(x, axis=-1), 0.0)
    x = x + _L0_gnn_ref(adj, h, L0_gnn_masked_x, L0_gnn_Wlq, L0_gnn_Wlk, L0_gnn_Wlv, L0_gnn_blv, L0_gnn_Wgq, L0_gnn_Wgk, L0_gnn_Wgv, L0_gnn_bgv, L0_gnn_Wes, L0_gnn_Wev, L0_gnn_bev)
    return x

_drawn_inputs = setup_inputs


def setup_inputs(seed=0):
    import zlib

    import numpy as np

    out = dict(_drawn_inputs(seed))
    spreads = {}
    factors = {'L0_gnn_blv': 8.0,
     'L0_gnn_Wgq': 4.893,
     'L0_gnn_Wgk': 5.133,
     'L0_gnn_Wgv': 2.667,
     'L0_gnn_bgv': 8.0,
     'L0_gnn_bev': 64.0}
    for name, (base, spread) in spreads.items():
        noise = np.random.default_rng([zlib.crc32(name.encode()), seed]).standard_normal(out[name].shape)
        drawn = base * np.exp(spread * noise) if base else spread * noise
        out[name] = jnp.asarray(drawn.astype(out[name].dtype))
    for name, factor in factors.items():
        out[name] = (out[name] * factor).astype(out[name].dtype)
    return out
```

```python
from contextlib import ExitStack

import concourse.bass as bass
from concourse import mybir

P = 128
F32, F16, U8, I32 = mybir.dt.float32, mybir.dt.float16, mybir.dt.uint8, mybir.dt.int32
ALU, ACT = mybir.AluOpType, mybir.ActivationFunctionType
AX_X = mybir.AxisListType.X

BLOCK = 512
CPB = BLOCK // P
H_SCALE = 2.0 ** 11
P_SCALE = 2.0 ** 15
Q_TOP = 2.0 ** 14
EPS = 1e-5
MASKED = 1e9
TINY = 1e-18


class Tile:

    def __init__(self, pair, offset):
        self.t = pair * 2 + offset
        self.par = offset % 2
        self.half = pair + offset // 2


def due(n):
    return not isinstance(n, int) or n > 0


def build(nc, x, adj, mxT, mx, WlqT, WlkT, Wlv, blv, WgqT, Wgk, Wgv, bgv, Wes, Wev, bev, out):
    N, D = x.shape
    T = N // P
    NB = N // BLOCK
    DC = D // P
    SCALE = float(D) ** -0.5
    MB = 4
    MW = N // MB
    BPM = MW // BLOCK

    x_groups = x.rearrange("(g j p) d -> g p j d", p=P, j=CPB)

    with ExitStack() as ctx:
        def sb(name, shape, dt=F32):
            return ctx.enter_context(nc.sbuf_tensor(name, shape, dt))

        def psum(name, shape, dt=F32):
            return ctx.enter_context(nc.psum_tensor(name, shape, dt))

        def sem(name):
            return ctx.enter_context(nc.semaphore(name))

        ps_scores = psum("ps_scores", [P, 2, BLOCK])
        ps_pT = psum("ps_pT", [P, 2, BLOCK])
        ps_u = psum("ps_u", [P, 2 * D])
        ps_q = psum("ps_q", [P, 2 * D])
        ps_fin = psum("ps_fin", [P, 2 * D])
        ps_small = psum("ps_small", [P, 2 * D])
        ps_gs = ps_small[:, 0:2]
        ps_qT = ps_small[:, D:2 * D].bitcast(F16)

        hT = sb("hT", [P, 2, DC, N], F16)
        h_rows = sb("h_rows", [P, N // P, 2 * D], F16)
        m_sb = sb("m_sb", [P, DC, D])
        wge = sb("wge", [P, DC, 2])
        wlv_sb = sb("wlv_sb", [P, DC, D])
        wev_sb = sb("wev_sb", [P, DC, D])
        blv_b = sb("blv_b", [P, D])
        bev_b = sb("bev_b", [P, D])
        gv_b = sb("gv_b", [P, D])
        ident16 = sb("ident16", [P, P], F16)
        ident32 = sb("ident32", [P, P])
        ones16 = sb("ones16", [P, 2], F16)
        ones32 = sb("ones32", [P, P])
        eps_sb = sb("eps_sb", [P, 1])

        xg = sb("xg", [P, 2, CPB, D])
        h32 = sb("h32", [P, 2, CPB, D])
        st6 = sb("st6", [P, 2, CPB, 6])
        mv = sb("mv", [P, 2, CPB, 2])
        sd = sb("sd", [P, 2, CPB])
        rs = sb("rs", [P, 2, CPB])
        rs_h = sb("rs_h", [P, 2, CPB])
        nb_h = sb("nb_h", [P, 2, CPB])
        wq_t = sb("wq_t", [P, DC, D])
        wk_t = sb("wk_t", [P, DC, D])
        wgq_t = sb("wgq_t", [P, DC, D])
        wgk_sb = sb("wgk_sb", [P, DC, D])
        wgv_sb = sb("wgv_sb", [P, DC, D])
        bgv_b = sb("bgv_b", [P, D])
        xbar_row = sb("xbar_row", [1, 2 * D])
        xbarT = sb("xbarT", [P, DC])
        xbar_bc = sb("xbar_bc", [P, DC, P])
        gk_u = sb("gk_u", [P, DC])

        adj8 = sb("adj8", [P, 2, N], U8)
        mxT_q = sb("mxT_q", [P, 2, DC, P])
        mxT_f = sb("mxT_f", [P, 2, DC, P])
        xm = sb("xm", [P, 2, 2, D])
        s32 = sb("s32", [P, 2, N])
        qT = sb("qT", [P, 2, 2 * DC, P], F16)
        invc = sb("invc", [P, 2])
        invc_x = sb("invc_x", [P, 2])
        big = sb("big", [P, 2, 2])
        gs_es = sb("gs_es", [P, 2, 2])
        bmax = sb("bmax", [P, 2, NB])
        negm = sb("negm", [P, 2])
        psums = sb("psums", [P, 2, NB])
        mass = sb("mass", [P, 2, 3])
        rows_done = sb("rows_done", [P, 2, D])
        o_sb = sb("o_sb", [P, 2, D])

        bias = sb("bias", [P, N])
        q_hl = sb("q_hl", [P, 2, D], F16)
        rmax = sb("rmax", [P, 1])
        rclamp = sb("rclamp", [P, 1])
        rpow = sb("rpow", [P, 1])
        cinv = sb("cinv", [P, 1])
        cq = sb("cq", [P, 1])
        mloc = sb("mloc", [P, 1])
        m1 = sb("m1", [P, 1])
        den = sb("den", [P, 1])
        rden = sb("rden", [P, 1])
        r_u = sb("r_u", [P, 1])
        w3 = sb("w3", [P, 3])
        u1 = sb("u1", [P, D])
        un = sb("un", [P, D])
        uT = sb("uT", [P, DC, P])
        e2 = sb("e2", [P, D])
        r1 = sb("r1", [P, D])
        r2 = sb("r2", [P, D])
        r3 = sb("r3", [P, D])
        pT_hi = sb("pT_hi", [P, 2, BLOCK], F16)
        pT_lo = sb("pT_lo", [P, 2, BLOCK], F16)

        s_x = [sem(f"s_x{i}") for i in range(2)]
        s_wqk, s_wg, s_wv, s_bc = sem("s_wqk"), sem("s_wg"), sem("s_wv"), sem("s_bc")
        s_adj = [sem(f"s_adj{i}") for i in range(2)]
        s_mxq = [sem(f"s_mxq{i}") for i in range(2)]
        s_mxf = [sem(f"s_mxf{i}") for i in range(2)]
        s_xm = [sem(f"s_xm{i}") for i in range(2)]
        s_out = [sem(f"s_out{i}") for i in range(2)]
        s_zero, s_ident, s_const = sem("s_zero"), sem("s_ident"), sem("s_const")
        s_bn, s_mv, s_sd, s_rs, s_rsh, s_nb = (sem(n) for n in ("s_bn", "s_mv", "s_sd", "s_rs", "s_rsh", "s_nb"))
        s_h, s_hhi, s_hlo = sem("s_h"), sem("s_hhi"), sem("s_hlo")
        s_hTps, s_hT_hi, s_hT_lo = sem("s_hTps"), sem("s_hT_hi"), sem("s_hT_lo")
        s_mps, s_m = sem("s_mps"), sem("s_m")
        s_xbar, s_gstep, s_gev = sem("s_xbar"), sem("s_gstep"), sem("s_gev")
        s_q, s_rowscale, s_cq, s_invc, s_big = sem("s_q"), sem("s_rowscale"), sem("s_cq"), sem("s_invc"), sem("s_big")
        s_qhi, s_qlo, s_qTps, s_qT = sem("s_qhi"), sem("s_qlo"), sem("s_qTps"), sem("s_qT")
        s_gs, s_gsc = sem("s_gs"), sem("s_gsc")
        s_bias, s_s, s_mask, s_mloc, s_negm = sem("s_bias"), sem("s_s"), sem("s_mask"), sem("s_mloc"), sem("s_negm")
        s_mask_go, s_bias_go = sem("s_mask_go"), sem("s_bias_go")
        s_exp, s_ge, s_pTps, s_phi, s_plo, s_pv = (sem(n) for n in ("s_exp", "s_ge", "s_pTps", "s_phi", "s_plo", "s_pv"))
        s_den, s_w, s_u1, s_un, s_uTps, s_uT, s_fin, s_res, s_o = (
            sem(n) for n in ("s_den", "s_w", "s_u1", "s_un", "s_uTps", "s_uT", "s_fin", "s_res", "s_o"))

        block = ctx.enter_context(nc.Block())

        def schedule(eng, step):
            def tiles(pair, o):
                return [Tile(pair, o + k) for k in (-1, 0, 1, 2, 3)]

            step(*tiles(0, 0), finish=False)
            step(*tiles(0, 1))
            with eng.Fori(0, (T - 4) // 2) as j:
                step(*tiles(j, 2))
                step(*tiles(j, 3))
            step(*tiles(0, T - 2), project=False)
            step(*tiles(0, T - 1), project=False, score=False)
            step(*tiles(0, T), project=False, score=False, weigh=False)

        @block.sync
        def _(sp):
            def load_x(g):
                if g >= 2:
                    sp.wait_ge(s_h, CPB * (g - 1))
                    sp.wait_ge(s_bn, CPB * (g - 1))
                sp.dma_start(xg[:, g % 2], x_groups[g]).then_inc(s_x[g % 2], 16)

            def load_adj(k):
                if due(k.t - 1):
                    sp.wait_ge(s_bias, (k.t - 1) * MB)
                sp.dma_start(adj8[:, k.par], adj[bass.ds(k.t * P, P), :]).then_inc(s_adj[k.par], 16)

            def load_mxT_q(k):
                if due(k.t - 1):
                    sp.wait_ge(s_q, k.t - 1)
                    sp.wait_ge(s_gs, k.t - 1)
                sp.dma_start(mxT_q[:, k.par], mxT[bass.ds(k.t, 1)].rearrange("a p c q -> (a p) c q")
                             ).then_inc(s_mxq[k.par], 16)

            def load_rows(k):
                if due(k.t - 1):
                    sp.wait_ge(s_fin, k.t - 1)
                sp.dma_start(mxT_f[:, k.par], mxT[bass.ds(k.t, 1)].rearrange("a p c q -> (a p) c q")
                             ).then_inc(s_mxf[k.par], 16)
                if due(k.t - 1):
                    sp.wait_ge(s_o, k.t - 1)
                sp.dma_start(xm[:, k.par, 0], x[bass.ds(k.t * P, P), :]).then_inc(s_xm[k.par], 16)
                sp.dma_start(xm[:, k.par, 1], mx[bass.ds(k.t * P, P), :]).then_inc(s_xm[k.par], 16)

            def cols(w):
                return w.rearrange("(c p) d -> p c d", p=P)

            load_x(0)
            sp.dma_start(wq_t[:, :, :], cols(WlqT)).then_inc(s_wqk, 16)
            sp.dma_start(wk_t[:, :, :], cols(WlkT)).then_inc(s_wqk, 16)
            load_mxT_q(Tile(0, 0))
            load_x(1)
            load_adj(Tile(0, 0))
            load_x(2)
            load_mxT_q(Tile(0, 1))
            load_x(3)
            for dst, src in ((wgq_t, WgqT), (wgk_sb, Wgk), (wgv_sb, Wgv)):
                sp.dma_start(dst[:, :, :], cols(src)).then_inc(s_wg, 16)
            with nc.allow_non_contiguous_dma(reason="a column of 256 words"):
                sp.dma_start(wge[:, :, 1:2], cols(Wes)).then_inc(s_wg, 16)
            load_x(4)
            for dst, src in ((wlv_sb, Wlv), (wev_sb, Wev)):
                sp.dma_start(dst[:, :, :], cols(src)).then_inc(s_wv, 16)
            for dst, src in ((blv_b, blv), (bev_b, bev), (bgv_b, bgv)):
                sp.dma_start(dst[:, :], src.partition_broadcast(P)).then_inc(s_bc, 16)
            load_x(5)
            load_adj(Tile(0, 1))
            load_x(6)
            load_x(7)
            load_adj(Tile(0, 2))
            load_mxT_q(Tile(0, 2))

            def step(prev, cur, nxt, nxt2, nxt3, finish=True, weigh=True, score=True, project=True):
                if weigh:
                    load_rows(cur)
                if project and (not isinstance(nxt3.t, int) or nxt3.t < T):
                    load_mxT_q(nxt3)
                    load_adj(nxt3)
                if finish:
                    sp.wait_ge(s_o, prev.t + 1)
                    sp.dma_start(out[bass.ds(prev.t * P, P), :], o_sb[:, prev.par]).then_inc(s_out[prev.par], 16)

            step(*[Tile(0, k) for k in (-1, 0, 1, 2, 3)], finish=False)
            step(*[Tile(0, k) for k in (0, 1, 2, 3, 4)])
            with sp.Fori(0, (T - 6) // 2) as j:
                step(*[Tile(j, 2 + k) for k in (-1, 0, 1, 2, 3)])
                step(*[Tile(j, 3 + k) for k in (-1, 0, 1, 2, 3)])
            for i in range(T - 4, T + 1):
                step(*[Tile(0, i + k) for k in (-1, 0, 1, 2, 3)], weigh=i < T)
            for par in range(2):
                sp.wait_ge(s_out[par], 16 * (T // 2))

        @block.gpsimd
        def _(pool):
            nc.gpsimd.memset(ident16[:, :], 0.0).then_inc(s_zero, 1)
            nc.gpsimd.memset(ident32[:, :], 0.0).then_inc(s_zero, 1)
            nc.gpsimd.memset(ones16[:, :], 1.0).then_inc(s_const, 1)
            nc.gpsimd.memset(ones32[:, :], 1.0).then_inc(s_const, 1)
            nc.gpsimd.memset(eps_sb[:, :], EPS).then_inc(s_const, 1)
            pool.wait_ge(s_zero, 2)
            for m in (ident16, ident32):
                nc.gpsimd.affine_select(out=m[:, :], in_=m[:, :], compare_op=ALU.not_equal, fill=1.0, base=0,
                                        pattern=[[-1, P]], channel_multiplier=1).then_inc(s_ident, 1)

            def h_low(g):
                pool.wait_ge(s_hhi, g + 1)
                nc.gpsimd.tensor_tensor(h_rows[:, g * CPB:(g + 1) * CPB, D:2 * D], h32[:, g % 2],
                                        h_rows[:, g * CPB:(g + 1) * CPB, 0:D], ALU.subtract).then_inc(s_hlo, 1)

            def mask_bias(k, b):
                if b == 0:
                    pool.wait_ge(s_adj[k.par], k.half * 16 + 16)
                    pool.wait_ge(s_big, k.t * 2 + 2)
                if due(k.t):
                    pool.wait_ge(s_mask, (k.t - 1) * NB + (b + 1) * BPM)
                pool.sem_inc(s_bias_go, 1)
                nc.gpsimd.tensor_scalar(bias[:, b * MW:(b + 1) * MW], adj8[:, k.par, b * MW:(b + 1) * MW],
                                        big[:, k.par, 0:1], big[:, k.par, 1:2], ALU.mult, ALU.add
                                        ).then_inc(s_bias, 1)

            def add_x(k):
                pool.wait_ge(s_res, k.t * 5 + 5)
                if due(k.t - 1):
                    pool.wait_ge(s_out[k.par], k.half * 16)
                pool.wait_ge(s_xm[k.par], k.half * 32 + 32)
                nc.gpsimd.tensor_tensor(o_sb[:, k.par], rows_done[:, k.par], xm[:, k.par, 0], ALU.add
                                        ).then_inc(s_o, 1)

            for g in range(NB):
                h_low(g)
                if g == 1:
                    for b in range(MB):
                        mask_bias(Tile(0, 0), b)
            for b in range(MB):
                mask_bias(Tile(0, 1), b)

            def step(prev, cur, nxt, nxt2, nxt3, finish=True, weigh=True, score=True, project=True):
                if project:
                    for b in range(MB - 1):
                        mask_bias(nxt2, b)
                if finish:
                    add_x(prev)
                if project:
                    mask_bias(nxt2, MB - 1)

            schedule(pool, step)

        @block.scalar
        def _(act):
            def h_apply(g):
                b = g % 2
                act.wait_ge(s_mv, CPB * (g + 1))
                if g == 0:
                    act.wait_ge(s_const, 3)
                if g >= 2:
                    act.wait_ge(s_rs, g - 1)
                nc.scalar.activation(sd[:, b], mv[:, b, :, 1], ACT.Sqrt, bias=eps_sb[:, 0:1]).then_inc(s_sd, 1)
                act.wait_ge(s_nb, g + 1)
                if g >= 2:
                    act.wait_ge(s_hlo, g - 1)
                for j in range(CPB):
                    nc.scalar.activation(h32[:, b, j], xg[:, b, j], ACT.Relu, bias=nb_h[:, b, j:j + 1],
                                         scale=rs_h[:, b, j:j + 1]).then_inc(s_h, 1)

            def hT_high_out(g):
                act.wait_ge(s_hTps, 2 * g + 1)
                nc.scalar.activation(hT[:, 0, :, g * BLOCK:(g + 1) * BLOCK],
                                     ps_pT[:, 0].bitcast(F16).rearrange("p (c k) -> p c k", c=DC),
                                     ACT.Copy).then_inc(s_hT_hi, 1)

            def qT_out(k):
                act.wait_ge(s_qTps, k.t + 1)
                if due(k.t - 1):
                    act.wait_ge(s_s, (k.t - 1) * NB)
                nc.scalar.activation(qT[:, k.par].rearrange("p c q -> p (c q)"), ps_qT, ACT.Copy).then_inc(s_qT, 1)

            def uT_out(k):
                act.wait_ge(s_uTps, k.t + 1)
                if due(k.t):
                    act.wait_ge(s_fin, k.t)
                nc.scalar.activation(uT[:, :, :].rearrange("p c q -> p (c q)"), ps_q[:, D:2 * D], ACT.Copy
                                     ).then_inc(s_uT, 1)

            def exp_block(k, b):
                nc.scalar.activation(s32[:, k.par, b * BLOCK:(b + 1) * BLOCK], s32[:, k.par, b * BLOCK:(b + 1) * BLOCK],
                                     ACT.Exp, bias=negm[:, k.par:k.par + 1], scale=invc_x[:, k.par:k.par + 1],
                                     accum_out=psums[:, k.par, b:b + 1]).then_inc(s_exp, 1)

            def p_high(k, b):
                n = k.t * NB + b
                act.wait_ge(s_pTps, n + 1)
                if due(n - 1):
                    act.wait_ge(s_pv, n - 1)
                nc.scalar.activation(pT_hi[:, b % 2], ps_pT[:, b % 2], ACT.Copy, scale=P_SCALE).then_inc(s_phi, 1)

            act.wait_ge(s_mps, 1)
            nc.scalar.activation(m_sb[:, :, :].rearrange("p c d -> p (c d)"), ps_fin[:, :], ACT.Copy, scale=SCALE
                                 ).then_inc(s_m, 1)
            for g in range(NB):
                h_apply(g)
                if g >= 1:
                    hT_high_out(g - 1)
                if g == 1:
                    qT_out(Tile(0, 0))
                if g == 5:
                    qT_out(Tile(0, 1))
            hT_high_out(NB - 1)

            def step(prev, cur, nxt, nxt2, nxt3, finish=True, weigh=True, score=True, project=True):
                if weigh:
                    act.wait_ge(s_negm, cur.t * 2 + 2)
                    if due(cur.t - 1):
                        act.wait_ge(s_w, (cur.t - 1) * 2)
                    nc.scalar.activation(mass[:, cur.par, 1:3], gs_es[:, cur.par], ACT.Exp,
                                         bias=negm[:, cur.par:cur.par + 1]).then_inc(s_ge, 1)
                    exp_block(cur, 0)
                for b in range(NB):
                    if weigh:
                        if b + 1 < NB:
                            exp_block(cur, b + 1)
                        p_high(cur, b)
                    if b == 3 and finish:
                        uT_out(prev)
                    if b == 4 and project:
                        qT_out(nxt2)

            schedule(act, step)

        @block.tensor
        def _(pe):
            def project(k):
                pe.wait_ge(s_mxq[k.par], k.half * 16 + 16)
                if due(k.t):
                    pe.wait_ge(s_qlo, k.t)
                if due(k.t - 3):
                    pe.wait_ge(s_uT, k.t - 3)
                for c in range(DC):
                    last = nc.tensor.matmul(ps_q[:, 0:D], mxT_q[:, k.par, c], m_sb[:, c], start=c == 0, stop=c == DC - 1)
                last.then_inc(s_q, 1)

            def side_scores(k):
                if due(k.t):
                    pe.wait_ge(s_gsc, k.t)
                if due(k.t - 1):
                    pe.wait_ge(s_qT, k.t)
                for c in range(DC):
                    last = nc.tensor.matmul(ps_gs, mxT_q[:, k.par, c], wge[:, c], start=c == 0, stop=c == DC - 1)
                last.then_inc(s_gs, 1)

            def q_transposes(k):
                pe.wait_ge(s_qlo, k.t + 1)
                if due(k.t):
                    pe.wait_ge(s_qT, k.t)
                if due(k.t - 1):
                    pe.wait_ge(s_gsc, k.t + 1)
                for hl in range(2):
                    for c in range(DC):
                        n = hl * DC + c
                        last = nc.tensor.transpose(ps_qT[:, n * P:(n + 1) * P], q_hl[:, hl, c * P:(c + 1) * P],
                                                   ident16[:, :])
                last.then_inc(s_qTps, 1)

            def scores(k, b):
                n = k.t * NB + b
                if b == 0:
                    pe.wait_ge(s_qT, k.t + 1)
                if due(n - 1):
                    pe.wait_ge(s_mask, n - 1)
                first = True
                for q_half, h_half in ((1, 0), (0, 1), (0, 0)):
                    for c in range(DC):
                        last = nc.tensor.matmul(ps_scores[:, b % 2], qT[:, k.par, q_half * DC + c],
                                                hT[:, h_half, c, b * BLOCK:(b + 1) * BLOCK],
                                                start=first, stop=q_half + h_half == 0 and c == DC - 1)
                        first = False
                last.then_inc(s_s, 1)

            def p_transposes(k, b):
                n = k.t * NB + b
                pe.wait_ge(s_exp, n + 1)
                if due(n - 1):
                    pe.wait_ge(s_plo, n - 1)
                for j in range(CPB):
                    at = b * BLOCK + j * P
                    last = nc.tensor.transpose(ps_pT[:, b % 2, j * P:(j + 1) * P], s32[:, k.par, at:at + P],
                                               ident32[:, :])
                last.then_inc(s_pTps, 1)

            def p_times_h(k, b):
                n = k.t * NB + b
                if b == 0 and due(k.t):
                    pe.wait_ge(s_un, k.t)
                pe.wait_ge(s_plo, n + 1)
                for j in range(CPB):
                    kc = b * CPB + j
                    nc.tensor.matmul(ps_u[:, :], pT_hi[:, b % 2, j * P:(j + 1) * P], h_rows[:, kc, :],
                                     start=kc == 0, stop=False)
                    last = nc.tensor.matmul(ps_u[:, 0:D], pT_lo[:, b % 2, j * P:(j + 1) * P], h_rows[:, kc, 0:D],
                                            start=False, stop=kc == NB * CPB - 1)
                last.then_inc(s_pv, 1)

            def u_transposes(k, project):
                pe.wait_ge(s_un, k.t + 1)
                pe.wait_ge(s_qlo, k.t + 4 if project else T)
                if due(k.t):
                    pe.wait_ge(s_uT, k.t)
                for c in range(DC):
                    last = nc.tensor.transpose(ps_q[:, D + c * P:D + (c + 1) * P], un[:, c * P:(c + 1) * P],
                                               ident32[:, :])
                last.then_inc(s_uTps, 1)

            def final(k):
                pe.wait_ge(s_mxf[k.par], k.half * 16 + 16)
                if due(k.t):
                    pe.wait_ge(s_res, (k.t - 1) * 5 + 2)
                for c in range(DC):
                    nc.tensor.matmul(ps_fin[:, D:2 * D], mxT_f[:, k.par, c], wev_sb[:, c], start=c == 0, stop=c == DC - 1)
                pe.wait_ge(s_uT, k.t + 1)
                for c in range(DC):
                    last = nc.tensor.matmul(ps_fin[:, 0:D], uT[:, c], wlv_sb[:, c], start=c == 0, stop=c == DC - 1)
                last.then_inc(s_fin, 1)

            def h_transposes(g):
                for hl in range(2):
                    if hl == 0:
                        pe.wait_ge(s_hhi, g + 1)
                        if g >= 1:
                            pe.wait_ge(s_hT_hi, g)
                    else:
                        pe.wait_ge(s_hlo, g + 1)
                        if g >= 1:
                            pe.wait_ge(s_hT_lo, g)
                    dst = ps_pT[:, hl].bitcast(F16)
                    for c in range(DC):
                        for j in range(CPB):
                            at = c * BLOCK + j * P
                            src = h_rows[:, g * CPB + j, hl * D + c * P:hl * D + (c + 1) * P]
                            last = nc.tensor.transpose(dst[:, at:at + P], src, ident16[:, :])
                    last.then_inc(s_hTps, 1)

            def mean_rows(g):
                for j in range(CPB):
                    kc = g * CPB + j
                    last = nc.tensor.matmul(ps_u[0:1, :], ones16[:, 0:1], h_rows[:, kc, :], start=kc == 0,
                                            stop=kc == NB * CPB - 1)
                if g == NB - 1:
                    last.then_inc(s_xbar, 1)

            pe.wait_ge(s_wqk, 32)
            for ic in range(DC):
                for c in range(DC):
                    last = nc.tensor.matmul(ps_fin[:, ic * D:(ic + 1) * D], wq_t[:, c, ic * P:(ic + 1) * P],
                                            wk_t[:, c], start=c == 0, stop=c == DC - 1)
            last.then_inc(s_mps, 1)
            pe.wait_ge(s_m, 1)
            project(Tile(0, 0))
            pe.wait_ge(s_ident, 2)
            pe.wait_ge(s_const, 2)
            for g in range(NB):
                h_transposes(g)
                mean_rows(g)
                if g == 0:
                    q_transposes(Tile(0, 0))
                if g == 3:
                    project(Tile(0, 1))
                if g == 4:
                    q_transposes(Tile(0, 1))
                if g >= 1:
                    pe.wait_ge(s_hT_hi, g)
                    pe.wait_ge(s_hT_lo, g)
                    scores(Tile(0, 0), g - 1)
            pe.wait_ge(s_hT_hi, NB)
            pe.wait_ge(s_hT_lo, NB)
            scores(Tile(0, 0), NB - 1)
            pe.wait_ge(s_gev, 1)
            pe.wait_ge(s_qT, 2)
            for c in range(DC):
                for hl in range(2):
                    last = nc.tensor.matmul(ps_small[:, c:c + 1], xbar_row[0:1, hl * D + c * P:hl * D + (c + 1) * P],
                                            ones32[0:1, 0:1], start=hl == 0, stop=hl == 1)
            last.then_inc(s_gstep, 1)
            pe.wait_ge(s_wg, 64)
            pe.wait_ge(s_gev, 2)
            for jc in range(DC):
                for c in range(DC):
                    last = nc.tensor.matmul(ps_small[:, 4 + jc:5 + jc], wgk_sb[:, c, jc * P:(jc + 1) * P],
                                            xbarT[:, c:c + 1], start=c == 0, stop=c == DC - 1)
            last.then_inc(s_gstep, 1)
            pe.wait_ge(s_gev, 3)
            for ic in range(DC):
                for c in range(DC):
                    last = nc.tensor.matmul(ps_small[:, 8 + ic:9 + ic], wgq_t[:, c, ic * P:(ic + 1) * P],
                                            gk_u[:, c:c + 1], start=c == 0, stop=c == DC - 1)
            last.then_inc(s_gstep, 1)
            pe.wait_ge(s_gev, 6)
            for c in range(DC):
                last = nc.tensor.matmul(ps_fin[:, 0:D], xbar_bc[:, c], wgv_sb[:, c], start=c == 0, stop=c == DC - 1)
            last.then_inc(s_gstep, 1)
            side_scores(Tile(0, 0))
            side_scores(Tile(0, 1))
            pe.wait_ge(s_gev, 7)

            def step(prev, cur, nxt, nxt2, nxt3, finish=True, weigh=True, score=True, project_=True):
                for b in range(NB):
                    if score:
                        scores(nxt, b)
                    if b == 0 and finish:
                        p_times_h(prev, NB - 1)
                    if weigh:
                        p_transposes(cur, b)
                        if b >= 1:
                            p_times_h(cur, b - 1)
                    if b == 0 and project_:
                        project(nxt2)
                        side_scores(nxt2)
                    if b == 3 and finish:
                        u_transposes(prev, project_)
                    if b == 5 and finish:
                        final(prev)
                    if b == 4 and project_:
                        q_transposes(nxt2)

            def step_(*a, project=True, **k):
                step(*a, project_=project, **k)

            schedule(pe, step_)

        @block.vector
        def _(dve):
            def h_stats(g):
                b = g % 2
                dve.wait_ge(s_x[b], 16 * (g // 2 + 1))
                for j in range(CPB):
                    nc.vector.bn_stats(st6[:, b, j], xg[:, b, j]).then_inc(s_bn, 1)
                for j in range(CPB):
                    dve.wait_ge(s_bn, CPB * g + j + 1)
                    nc.vector.bn_aggr(mv[:, b, j], st6[:, b, j]).then_inc(s_mv, 1)

            def h_scales(g):
                b = g % 2
                dve.wait_ge(s_sd, g + 1)
                nc.vector.reciprocal(rs[:, b], sd[:, b]).then_inc(s_rs, 1)
                dve.wait_ge(s_rs, g + 1)
                if g >= 2:
                    dve.wait_ge(s_h, CPB * (g - 1))
                nc.vector.tensor_scalar(rs_h[:, b], rs[:, b], H_SCALE, None, ALU.mult).then_inc(s_rsh, 1)
                dve.wait_ge(s_rsh, g + 1)
                dve.wait_ge(s_mv, CPB * (g + 1))
                nc.vector.scalar_tensor_tensor(nb_h[:, b], mv[:, b, :, 0], -1.0, rs_h[:, b], ALU.mult, ALU.mult
                                               ).then_inc(s_nb, 1)

            def h_high(g):
                dve.wait_ge(s_h, CPB * (g + 1))
                nc.vector.tensor_copy(h_rows[:, g * CPB:(g + 1) * CPB, 0:D], h32[:, g % 2]).then_inc(s_hhi, 1)

            def hT_low_out(g):
                dve.wait_ge(s_hTps, 2 * g + 2)
                nc.vector.tensor_copy(hT[:, 1, :, g * BLOCK:(g + 1) * BLOCK],
                                      ps_pT[:, 1].bitcast(F16).rearrange("p (c k) -> p c k", c=DC)
                                      ).then_inc(s_hT_lo, 1)

            def q_split(k):
                dve.wait_ge(s_q, k.t + 1)
                nc.vector.tensor_reduce(rmax[:, :], ps_q[:, 0:D], AX_X, ALU.max, apply_absolute_value=True
                                        ).then_inc(s_rowscale, 1)
                dve.wait_ge(s_rowscale, k.t * 4 + 1)
                nc.vector.tensor_scalar(rclamp[:, :], rmax[:, :], TINY, None, ALU.max).then_inc(s_rowscale, 1)
                dve.wait_ge(s_rowscale, k.t * 4 + 2)
                nc.vector.tensor_scalar(rpow[:, :].bitcast(I32), rclamp[:, :].bitcast(I32), 0x7F800000, None,
                                        ALU.bitwise_and).then_inc(s_rowscale, 1)
                dve.wait_ge(s_rowscale, k.t * 4 + 3)
                nc.vector.tensor_scalar(cinv[:, :], rpow[:, :], 1.0 / Q_TOP, None, ALU.mult).then_inc(s_rowscale, 1)
                nc.vector.tensor_scalar(invc[:, k.par:k.par + 1], rpow[:, :], 1.0 / (Q_TOP * H_SCALE), None, ALU.mult
                                        ).then_inc(s_invc, 1)
                dve.wait_ge(s_rowscale, k.t * 4 + 4)
                nc.vector.reciprocal(cq[:, :], cinv[:, :]).then_inc(s_cq, 1)
                dve.wait_ge(s_cq, k.t + 1)
                if due(k.t):
                    dve.wait_ge(s_qTps, k.t)
                nc.vector.tensor_scalar(q_hl[:, 0], ps_q[:, 0:D], cq[:, 0:1], None, ALU.mult).then_inc(s_qhi, 1)
                if due(k.t - 1):
                    dve.wait_ge(s_bias, (k.t - 1) * MB)
                for n, sign in enumerate((1.0, -1.0)):
                    nc.vector.tensor_scalar(big[:, k.par, n:n + 1], cq[:, :], sign * MASKED * H_SCALE, None, ALU.mult
                                            ).then_inc(s_big, 1)
                dve.wait_ge(s_qhi, k.t + 1)
                nc.vector.scalar_tensor_tensor(q_hl[:, 1], ps_q[:, 0:D], cq[:, 0:1], q_hl[:, 0], ALU.mult, ALU.subtract
                                               ).then_inc(s_qlo, 1)

            def side_out(k):
                dve.wait_ge(s_gs, k.t + 1)
                if due(k.t - 1):
                    dve.wait_ge(s_ge, k.t - 1)
                nc.vector.tensor_copy(gs_es[:, k.par], ps_gs).then_inc(s_gsc, 1)

            def add_mask(k, b):
                n = k.t * NB + b
                if b % BPM == 0:
                    dve.wait_ge(s_bias, k.t * MB + b // BPM + 1)
                dve.wait_ge(s_s, n + 1)
                if due(k.t - 1):
                    dve.wait_ge(s_pTps, (k.t - 2) * NB + b + 1)
                dve.sem_inc(s_mask_go, 1)
                nc.vector.tensor_tensor_reduce(
                    out=s32[:, k.par, b * BLOCK:(b + 1) * BLOCK], in0=ps_scores[:, b % 2],
                    in1=bias[:, b * BLOCK:(b + 1) * BLOCK], scale=1.0, scalar=-3.0e38, op0=ALU.add, op1=ALU.max,
                    accum_out=bmax[:, k.par, b:b + 1]).then_inc(s_mask, 1)

            def row_max(k):
                par = slice(k.par, k.par + 1)
                dve.wait_ge(s_mask, (k.t + 1) * NB)
                dve.wait_ge(s_gsc, k.t + 1)
                dve.wait_ge(s_invc, k.t + 1)
                nc.vector.reduce_max(mloc[:, :], bmax[:, k.par], AX_X).then_inc(s_mloc, 1)
                if due(k.t - 1):
                    dve.wait_ge(s_exp, (k.t - 1) * NB)
                nc.vector.tensor_copy(invc_x[:, par], invc[:, par]).then_inc(s_negm, 1)
                dve.wait_ge(s_mloc, k.t * 2 + 1)
                nc.vector.tensor_scalar(m1[:, :], mloc[:, :], invc[:, par], gs_es[:, k.par, 0:1], ALU.mult, ALU.max
                                        ).then_inc(s_mloc, 1)
                dve.wait_ge(s_mloc, k.t * 2 + 2)
                nc.vector.tensor_scalar(negm[:, par], m1[:, :], gs_es[:, k.par, 1:2], -1.0, ALU.max, ALU.mult
                                        ).then_inc(s_negm, 1)

            def p_low(k, b):
                n = k.t * NB + b
                dve.wait_ge(s_phi, n + 1)
                if due(n - 1):
                    dve.wait_ge(s_pv, n - 1)
                nc.vector.scalar_tensor_tensor(pT_lo[:, b % 2], ps_pT[:, b % 2], P_SCALE, pT_hi[:, b % 2],
                                               ALU.mult, ALU.subtract).then_inc(s_plo, 1)

            def weights(k):
                dve.wait_ge(s_exp, (k.t + 1) * NB)
                dve.wait_ge(s_ge, k.t + 1)
                nc.vector.reduce_sum(mass[:, k.par, 0:1], psums[:, k.par], AX_X).then_inc(s_den, 1)
                dve.wait_ge(s_den, k.t * 3 + 1)
                nc.vector.reduce_sum(den[:, :], mass[:, k.par], AX_X).then_inc(s_den, 1)
                dve.wait_ge(s_den, k.t * 3 + 2)
                nc.vector.reciprocal(rden[:, :], den[:, :]).then_inc(s_den, 1)
                dve.wait_ge(s_den, k.t * 3 + 3)
                nc.vector.tensor_scalar(r_u[:, :], rden[:, :], 1.0 / (P_SCALE * H_SCALE), None, ALU.mult
                                        ).then_inc(s_w, 1)
                nc.vector.tensor_scalar(w3[:, :], mass[:, k.par], rden[:, 0:1], None, ALU.mult).then_inc(s_w, 1)

            def u_out(k):
                dve.wait_ge(s_w, k.t * 2 + 2)
                dve.wait_ge(s_pv, (k.t + 1) * NB)
                nc.vector.tensor_scalar(u1[:, :], ps_u[:, D:2 * D], r_u[:, 0:1], None, ALU.mult).then_inc(s_u1, 1)
                dve.wait_ge(s_u1, k.t + 1)
                if due(k.t):
                    dve.wait_ge(s_uTps, k.t)
                nc.vector.scalar_tensor_tensor(un[:, :], ps_u[:, 0:D], r_u[:, 0:1], u1[:, :], ALU.mult, ALU.add
                                               ).then_inc(s_un, 1)

            def combine(k):
                dve.wait_ge(s_fin, k.t + 1)
                nc.vector.tensor_tensor(e2[:, :], ps_fin[:, D:2 * D], bev_b[:, :], ALU.add).then_inc(s_res, 1)
                dve.wait_ge(s_res, k.t * 5 + 1)
                nc.vector.scalar_tensor_tensor(r1[:, :], e2[:, :], w3[:, 2:3], ps_fin[:, 0:D], ALU.mult, ALU.add
                                               ).then_inc(s_res, 1)
                dve.wait_ge(s_res, k.t * 5 + 2)
                nc.vector.scalar_tensor_tensor(r2[:, :], blv_b[:, :], w3[:, 0:1], r1[:, :], ALU.mult, ALU.add
                                               ).then_inc(s_res, 1)
                dve.wait_ge(s_res, k.t * 5 + 3)
                nc.vector.scalar_tensor_tensor(r3[:, :], gv_b[:, :], w3[:, 1:2], r2[:, :], ALU.mult, ALU.add
                                               ).then_inc(s_res, 1)
                dve.wait_ge(s_res, k.t * 5 + 4)
                dve.wait_ge(s_xm[k.par], k.half * 32 + 32)
                if due(k.t - 1):
                    dve.wait_ge(s_o, k.t - 1)
                nc.vector.tensor_tensor(rows_done[:, k.par], r3[:, :], xm[:, k.par, 1], ALU.max).then_inc(s_res, 1)

            for g in range(NB):
                h_stats(g)
                h_scales(g)
                if g == 1:
                    q_split(Tile(0, 0))
                if g == 5:
                    q_split(Tile(0, 1))
                h_high(g)
                if g >= 1:
                    hT_low_out(g - 1)
                if g >= 2:
                    add_mask(Tile(0, 0), g - 2)
            hT_low_out(NB - 1)
            add_mask(Tile(0, 0), NB - 2)
            dve.wait_ge(s_xbar, 1)
            nc.vector.tensor_scalar(xbar_row[:, :], ps_u[0:1, :], 1.0 / (N * H_SCALE), None, ALU.mult).then_inc(s_gev, 1)
            add_mask(Tile(0, 0), NB - 1)
            dve.wait_ge(s_gstep, 1)
            nc.vector.tensor_copy(xbarT[:, :], ps_small[:, 0:DC]).then_inc(s_gev, 1)
            dve.wait_ge(s_gstep, 2)
            nc.vector.tensor_copy(gk_u[:, :], ps_small[:, 4:4 + DC]).then_inc(s_gev, 1)
            dve.wait_ge(s_gstep, 3)
            dve.wait_ge(s_wg, 64)
            nc.vector.tensor_scalar(wge[:, :, 0], ps_small[:, 8:8 + DC], SCALE, None, ALU.mult).then_inc(s_gev, 1)
            dve.wait_ge(s_gev, 2)
            for c in range(DC):
                nc.vector.tensor_scalar(xbar_bc[:, c], ones32[:, :], xbarT[:, c:c + 1], None, ALU.mult
                                        ).then_inc(s_gev, 1)
            dve.wait_ge(s_gstep, 4)
            dve.wait_ge(s_bc, 48)
            nc.vector.tensor_tensor(gv_b[:, :], ps_fin[:, 0:D], bgv_b[:, :], ALU.add).then_inc(s_gev, 1)
            side_out(Tile(0, 0))
            side_out(Tile(0, 1))
            row_max(Tile(0, 0))

            def step(prev, cur, nxt, nxt2, nxt3, finish=True, weigh=True, score=True, project=True):
                if finish:
                    weights(prev)
                for b in range(NB):
                    if score:
                        add_mask(nxt, b)
                    if b == 0 and finish:
                        u_out(prev)
                    if weigh:
                        p_low(cur, b)
                    if b == 1 and project:
                        q_split(nxt2)
                        side_out(nxt2)
                    if b == 6 and finish:
                        combine(prev)
                if score:
                    row_max(nxt)

            schedule(dve, step)


def kernel(x, adj, L0_gnn_masked_x, L0_gnn_Wlq, L0_gnn_Wlk, L0_gnn_Wlv, L0_gnn_blv, L0_gnn_Wgq, L0_gnn_Wgk,
           L0_gnn_Wgv, L0_gnn_bgv, L0_gnn_Wes, L0_gnn_Wev, L0_gnn_bev):
    import numpy as np
    import concourse.bacc as bacc
    from concourse.bass_utils import run_bass_kernel_spmd as run

    mx = np.asarray(L0_gnn_masked_x)
    N, D = mx.shape
    arrays = {
        "x": np.asarray(x),
        "adj": np.asarray(adj),
        "mxT": mx.reshape(N // P, P, D // P, P).transpose(0, 3, 2, 1),
        "mx": mx,
        "WlqT": np.asarray(L0_gnn_Wlq).T,
        "WlkT": np.asarray(L0_gnn_Wlk).T,
        "Wlv": np.asarray(L0_gnn_Wlv),
        "blv": np.asarray(L0_gnn_blv),
        "WgqT": np.asarray(L0_gnn_Wgq).T,
        "Wgk": np.asarray(L0_gnn_Wgk),
        "Wgv": np.asarray(L0_gnn_Wgv),
        "bgv": np.asarray(L0_gnn_bgv),
        "Wes": np.asarray(L0_gnn_Wes),
        "Wev": np.asarray(L0_gnn_Wev),
        "bev": np.asarray(L0_gnn_bev),
    }
    arrays = {name: np.ascontiguousarray(a) for name, a in arrays.items()}
    nc = bacc.Bacc("TRN2", target_bir_lowering=False, num_devices=1)
    args = [nc.dram_tensor(name, a.shape, mybir.dt.from_np(a.dtype), kind="ExternalInput").ap()
            for name, a in arrays.items()]
    args.append(nc.dram_tensor("out", (N, D), F32, kind="ExternalOutput").ap())
    build(nc, *args)
    return run(nc, [arrays], core_ids=[0]).results[0]["out"]
```

```python
from contextlib import ExitStack

import concourse.bass as bass
from concourse import mybir

P = 128
F32, F16, U8, I32 = mybir.dt.float32, mybir.dt.float16, mybir.dt.uint8, mybir.dt.int32
ALU, ACT = mybir.AluOpType, mybir.ActivationFunctionType
AX_X = mybir.AxisListType.X

BLOCK = 512
CPB = BLOCK // P
H_SCALE = 2.0 ** 11
P_SCALE = 2.0 ** 15
Q_TOP = 2.0 ** 14
EPS = 1e-5
MASKED = 1e9
TINY = 1e-18


class Tile:

    def __init__(self, pair, offset):
        self.t = pair * 2 + offset
        self.par = offset % 2
        self.half = pair + offset // 2


def due(n):
    return not isinstance(n, int) or n > 0


def build(nc, x, adj, mxT, mx, WlqT, WlkT, Wlv, blv, WgqT, Wgk, Wgv, bgv, Wes, Wev, bev, out):
    N, D = x.shape
    T = N // P
    NB = N // BLOCK
    DC = D // P
    SCALE = float(D) ** -0.5
    MB = 4
    MW = N // MB
    BPM = MW // BLOCK
    BPU = 2
    NU = NB // BPU
    LAG = 4
    XG = 4

    x_groups = x.rearrange("(g j p) d -> g p j d", p=P, j=CPB)

    with ExitStack() as ctx:
        def sb(name, shape, dt=F32):
            return ctx.enter_context(nc.sbuf_tensor(name, shape, dt))

        def psum(name, shape, dt=F32):
            return ctx.enter_context(nc.psum_tensor(name, shape, dt))

        def sem(name):
            return ctx.enter_context(nc.semaphore(name))

        ps_scores = psum("ps_scores", [P, 2, BLOCK])
        ps_u = psum("ps_u", [P, 2, 2 * D])
        ps_q = psum("ps_q", [P, 2 * D])
        ps_uT = psum("ps_uT", [P, 2 * D])
        ps_fin = psum("ps_fin", [P, 2 * D])
        ps_small = psum("ps_small", [P, 2 * D])
        ps_gs = ps_small[:, 0:2]

        hT = sb("hT", [P, N // P, 2 * DC, P], F16)
        h_rows = sb("h_rows", [P, N // P, 2 * D], F16)
        m_sb = sb("m_sb", [P, DC, D])
        wge = sb("wge", [P, DC, 2])
        wlv_sb = sb("wlv_sb", [P, DC, D])
        wev_sb = sb("wev_sb", [P, DC, D])
        blv_b = sb("blv_b", [P, D])
        bev_b = sb("bev_b", [P, D])
        gv_b = sb("gv_b", [P, D])
        ident32 = sb("ident32", [P, P])
        ones16 = sb("ones16", [P, 2], F16)
        ones32 = sb("ones32", [P, P])
        eps_sb = sb("eps_sb", [P, 1])

        shared = sb("shared", [P, XG * CPB * D])
        xg = shared[:, :].rearrange("p (g j d) -> p g j d", g=XG, j=CPB)
        h32 = sb("h32", [P, 2, CPB, D])
        st6 = sb("st6", [P, 2, CPB, 6])
        mv = sb("mv", [P, 2, CPB, 2])
        sd = sb("sd", [P, 2, CPB])
        rs = sb("rs", [P, 2, CPB])
        rs_h = sb("rs_h", [P, 2, CPB])
        nb_h = sb("nb_h", [P, 2, CPB])
        wq_t = sb("wq_t", [P, DC, D])
        wk_t = sb("wk_t", [P, DC, D])
        wgq_t = sb("wgq_t", [P, DC, D])
        wgk_sb = sb("wgk_sb", [P, DC, D])
        wgv_sb = sb("wgv_sb", [P, DC, D])
        bgv_b = sb("bgv_b", [P, D])
        xbar_row = sb("xbar_row", [1, 2 * D])
        xbarT = sb("xbarT", [P, DC])
        xbar_bc = sb("xbar_bc", [P, DC, P])
        gk_u = sb("gk_u", [P, DC])

        adj8 = sb("adj8", [P, 2, N], U8)
        mxT_q = sb("mxT_q", [P, 2, DC, P])
        mxT_f = sb("mxT_f", [P, 2, DC, P])
        xm = sb("xm", [P, 2, 2, D])
        s32 = sb("s32", [P, 2, N])
        qT = sb("qT", [P, 2, 2 * DC, P], F16)
        q_hl = sb("q_hl", [P, 2, 2, D], F16)
        invc = sb("invc", [P, 2])
        invc_x = sb("invc_x", [P, 2])
        big = sb("big", [P, 2, 2])
        gs_es = sb("gs_es", [P, 2, 2])
        bmax = sb("bmax", [P, 2, NB])
        negm = sb("negm", [P, 2])
        psums = sb("psums", [P, 2, NB])
        mass = sb("mass", [P, 2, 3])
        rows_done = sb("rows_done", [P, 2, D])
        o_sb = sb("o_sb", [P, 2, D])

        bias = sb("bias", [P, N])
        rmax = sb("rmax", [P, 1])
        rclamp = sb("rclamp", [P, 1])
        rpow = sb("rpow", [P, 1])
        cinv = sb("cinv", [P, 1])
        cq = sb("cq", [P, 1])
        mloc = sb("mloc", [P, 1])
        m1 = sb("m1", [P, 1])
        den = sb("den", [P, 1])
        rden = sb("rden", [P, 1])
        r_u = sb("r_u", [P, 1])
        w3 = sb("w3", [P, 3])
        u1 = sb("u1", [P, D])
        un = sb("un", [P, D])
        uT = sb("uT", [P, DC, P])
        e2 = sb("e2", [P, D])
        r1 = sb("r1", [P, D])
        r2 = sb("r2", [P, D])
        r3 = sb("r3", [P, D])
        p_hl = sb("p_hl", [P, 2, 2, BPU * BLOCK], F16)
        pT = shared[:, :].bitcast(F16).rearrange(
            "p (u a c q) -> p u a c q", u=NU, a=2, q=P)

        s_x = [sem(f"s_x{i}") for i in range(XG)]
        s_hT = [sem(f"s_hT{i}") for i in range(XG)]
        s_qT = [sem(f"s_qT{i}") for i in range(2)]
        s_pT = [sem(f"s_pT{i}") for i in range(NU)]
        s_wqk, s_wg, s_wv, s_bc = sem("s_wqk"), sem("s_wg"), sem("s_wv"), sem("s_bc")
        s_adj = [sem(f"s_adj{i}") for i in range(2)]
        s_mxq = [sem(f"s_mxq{i}") for i in range(2)]
        s_mxf = [sem(f"s_mxf{i}") for i in range(2)]
        s_xm = [sem(f"s_xm{i}") for i in range(2)]
        s_out = [sem(f"s_out{i}") for i in range(2)]
        s_zero, s_ident, s_const = sem("s_zero"), sem("s_ident"), sem("s_const")
        s_bn, s_mv, s_sd, s_rs, s_rsh, s_nb = (sem(n) for n in ("s_bn", "s_mv", "s_sd", "s_rs", "s_rsh", "s_nb"))
        s_h, s_hhi, s_hlo = sem("s_h"), sem("s_hhi"), sem("s_hlo")
        s_mps, s_m = sem("s_mps"), sem("s_m")
        s_xbar, s_gstep, s_gev = sem("s_xbar"), sem("s_gstep"), sem("s_gev")
        s_q, s_rowscale, s_cq, s_invc, s_big = sem("s_q"), sem("s_rowscale"), sem("s_cq"), sem("s_invc"), sem("s_big")
        s_qhi, s_qlo = sem("s_qhi"), sem("s_qlo")
        s_gs, s_gsc = sem("s_gs"), sem("s_gsc")
        s_bias, s_s, s_mask, s_mloc, s_negm = sem("s_bias"), sem("s_s"), sem("s_mask"), sem("s_mloc"), sem("s_negm")
        s_mask_go, s_bias_go, s_sp_go = sem("s_mask_go"), sem("s_bias_go"), sem("s_sp_go")
        s_exp, s_ge, s_phi, s_plo, s_pv = (sem(n) for n in ("s_exp", "s_ge", "s_phi", "s_plo", "s_pv"))
        s_den, s_w, s_u1, s_un, s_uTps, s_uT, s_fin, s_res, s_o = (
            sem(n) for n in ("s_den", "s_w", "s_u1", "s_un", "s_uTps", "s_uT", "s_fin", "s_res", "s_o"))

        block = ctx.enter_context(nc.Block())

        def schedule(eng, step):
            def tiles(pair, o):
                return [Tile(pair, o + k) for k in (-1, 0, 1, 2, 3)]

            step(*tiles(0, 0), finish=False)
            step(*tiles(0, 1))
            with eng.Fori(0, (T - 4) // 2) as j:
                step(*tiles(j, 2))
                step(*tiles(j, 3))
            step(*tiles(0, T - 2), project=False)
            step(*tiles(0, T - 1), project=False, score=False)
            step(*tiles(0, T), project=False, score=False, weigh=False)

        def carry(sp):
            sp.sem_inc(s_sp_go, 1)

        @block.sync
        def _(sp):
            def load_x(g):
                if g >= XG:
                    sp.wait_ge(s_h, CPB * (g - XG + 1))
                    sp.wait_ge(s_bn, CPB * (g - XG + 1))
                sp.dma_start(xg[:, g % XG], x_groups[g]).then_inc(s_x[g % XG], 16)

            def transpose_h(g):
                sp.wait_ge(s_hhi, g + 1)
                sp.wait_ge(s_hlo, g + 1)
                sp.dma_start_transpose(
                    hT[:, g * CPB:(g + 1) * CPB].rearrange("p k c q -> p (k c) q"),
                    h_rows[:, g * CPB:(g + 1) * CPB].rearrange("p k d -> p (k d)")).then_inc(s_hT[g % XG], 16)

            def transpose_q(k):
                sp.wait_ge(s_qlo, k.t + 1)
                carry(sp)
                if due(k.t - 1):
                    sp.wait_ge(s_s, (k.t - 1) * NB)
                    carry(sp)
                sp.dma_start_transpose(qT[:, k.par], q_hl[:, k.par].rearrange("p a d -> p (a d)")
                                       ).then_inc(s_qT[k.par], 16)

            def transpose_p(k, u):
                sp.wait_ge(s_plo, k.t * NB + (u + 1) * BPU)
                carry(sp)
                if due(k.t):
                    sp.wait_ge(s_pv, (k.t - 1) * NB + (u + 1) * BPU)
                    carry(sp)
                sp.dma_start_transpose(pT[:, u].rearrange("p a c q -> p (a c) q"),
                                       p_hl[:, u % 2].rearrange("p a k -> p (a k)")).then_inc(s_pT[u], 16)

            def load_adj(k):
                if due(k.t - 1):
                    sp.wait_ge(s_bias, (k.t - 1) * MB)
                    carry(sp)
                sp.dma_start(adj8[:, k.par], adj[bass.ds(k.t * P, P), :]).then_inc(s_adj[k.par], 16)

            def load_mxT_q(k):
                if due(k.t - 1):
                    sp.wait_ge(s_q, k.t - 1)
                    carry(sp)
                    sp.wait_ge(s_gs, k.t - 1)
                    carry(sp)
                sp.dma_start(mxT_q[:, k.par], mxT[bass.ds(k.t, 1)].rearrange("a p c q -> (a p) c q")
                             ).then_inc(s_mxq[k.par], 16)

            def load_rows(k):
                if due(k.t - 1):
                    sp.wait_ge(s_fin, k.t - 1)
                    carry(sp)
                sp.dma_start(mxT_f[:, k.par], mxT[bass.ds(k.t, 1)].rearrange("a p c q -> (a p) c q")
                             ).then_inc(s_mxf[k.par], 16)
                if due(k.t - 1):
                    sp.wait_ge(s_o, k.t - 1)
                    carry(sp)
                sp.dma_start(xm[:, k.par, 0], x[bass.ds(k.t * P, P), :]).then_inc(s_xm[k.par], 16)
                sp.dma_start(xm[:, k.par, 1], mx[bass.ds(k.t * P, P), :]).then_inc(s_xm[k.par], 16)

            def cols(w):
                return w.rearrange("(c p) d -> p c d", p=P)

            load_x(0)
            sp.dma_start(wq_t[:, :, :], cols(WlqT)).then_inc(s_wqk, 16)
            sp.dma_start(wk_t[:, :, :], cols(WlkT)).then_inc(s_wqk, 16)
            load_x(1)
            load_mxT_q(Tile(0, 0))
            load_x(2)
            load_adj(Tile(0, 0))
            load_x(3)
            load_mxT_q(Tile(0, 1))
            for g in range(NB):
                if g == 1:
                    transpose_q(Tile(0, 0))
                transpose_h(g)
                if g + XG < NB:
                    load_x(g + XG)
                if g == 0:
                    for dst, src in ((wgq_t, WgqT), (wgk_sb, Wgk), (wgv_sb, Wgv)):
                        sp.dma_start(dst[:, :, :], cols(src)).then_inc(s_wg, 16)
                    with nc.allow_non_contiguous_dma(reason="a column of 256 words"):
                        sp.dma_start(wge[:, :, 1:2], cols(Wes)).then_inc(s_wg, 16)
                    load_adj(Tile(0, 1))
                if g == 2:
                    for dst, src in ((wlv_sb, Wlv), (wev_sb, Wev)):
                        sp.dma_start(dst[:, :, :], cols(src)).then_inc(s_wv, 16)
                    for dst, src in ((blv_b, blv), (bev_b, bev), (bgv_b, bgv)):
                        sp.dma_start(dst[:, :], src.partition_broadcast(P)).then_inc(s_bc, 16)
                if g == 6:
                    transpose_q(Tile(0, 1))
            load_adj(Tile(0, 2))
            load_mxT_q(Tile(0, 2))

            def step(prev, cur, nxt, nxt2, nxt3, finish=True, weigh=True, project=True):
                if weigh:
                    load_rows(cur)
                    transpose_p(cur, 0)
                if project:
                    transpose_q(nxt2)
                if weigh:
                    transpose_p(cur, 1)
                if project and (not isinstance(nxt3.t, int) or nxt3.t < T):
                    load_mxT_q(nxt3)
                    load_adj(nxt3)
                if weigh:
                    transpose_p(cur, 2)
                    transpose_p(cur, 3)
                if finish:
                    sp.wait_ge(s_o, prev.t + 1)
                    carry(sp)
                    sp.dma_start(out[bass.ds(prev.t * P, P), :], o_sb[:, prev.par]).then_inc(s_out[prev.par], 16)

            step(*[Tile(0, k) for k in (-1, 0, 1, 2, 3)], finish=False)
            step(*[Tile(0, k) for k in (0, 1, 2, 3, 4)])
            with sp.Fori(0, (T - 6) // 2) as j:
                step(*[Tile(j, 2 + k) for k in (-1, 0, 1, 2, 3)])
                step(*[Tile(j, 3 + k) for k in (-1, 0, 1, 2, 3)])
            for i in range(T - 4, T + 1):
                step(*[Tile(0, i + k) for k in (-1, 0, 1, 2, 3)], weigh=i < T, project=i + 2 < T)
            for par in range(2):
                sp.wait_ge(s_out[par], 16 * (T // 2))

        @block.gpsimd
        def _(pool):
            nc.gpsimd.memset(ident32[:, :], 0.0).then_inc(s_zero, 1)
            nc.gpsimd.memset(ones16[:, :], 1.0).then_inc(s_const, 1)
            nc.gpsimd.memset(ones32[:, :], 1.0).then_inc(s_const, 1)
            nc.gpsimd.memset(eps_sb[:, :], EPS).then_inc(s_const, 1)
            pool.wait_ge(s_zero, 1)
            nc.gpsimd.affine_select(out=ident32[:, :], in_=ident32[:, :], compare_op=ALU.not_equal, fill=1.0, base=0,
                                    pattern=[[-1, P]], channel_multiplier=1).then_inc(s_ident, 1)

            def h_low(g):
                pool.wait_ge(s_hhi, g + 1)
                nc.gpsimd.tensor_tensor(h_rows[:, g * CPB:(g + 1) * CPB, D:2 * D], h32[:, g % 2],
                                        h_rows[:, g * CPB:(g + 1) * CPB, 0:D], ALU.subtract).then_inc(s_hlo, 1)

            def mask_bias(k, b):
                if b == 0:
                    pool.wait_ge(s_adj[k.par], k.half * 16 + 16)
                    pool.wait_ge(s_big, k.t * 2 + 2)
                if due(k.t):
                    pool.wait_ge(s_mask, (k.t - 1) * NB + (b + 1) * BPM)
                pool.sem_inc(s_bias_go, 1)
                nc.gpsimd.tensor_scalar(bias[:, b * MW:(b + 1) * MW], adj8[:, k.par, b * MW:(b + 1) * MW],
                                        big[:, k.par, 0:1], big[:, k.par, 1:2], ALU.mult, ALU.add
                                        ).then_inc(s_bias, 1)

            def add_x(k):
                pool.wait_ge(s_res, k.t * 5 + 5)
                if due(k.t - 1):
                    pool.wait_ge(s_out[k.par], k.half * 16)
                pool.wait_ge(s_xm[k.par], k.half * 32 + 32)
                nc.gpsimd.tensor_tensor(o_sb[:, k.par], rows_done[:, k.par], xm[:, k.par, 0], ALU.add
                                        ).then_inc(s_o, 1)

            for g in range(NB):
                h_low(g)
                if g == 1:
                    for b in range(MB):
                        mask_bias(Tile(0, 0), b)
            for b in range(MB):
                mask_bias(Tile(0, 1), b)

            def step(prev, cur, nxt, nxt2, nxt3, finish=True, weigh=True, score=True, project=True):
                if project:
                    for b in range(MB - 1):
                        mask_bias(nxt2, b)
                if finish:
                    add_x(prev)
                if project:
                    mask_bias(nxt2, MB - 1)

            schedule(pool, step)

        @block.scalar
        def _(act):
            def h_apply(g):
                b = g % 2
                act.wait_ge(s_mv, CPB * (g + 1))
                if g == 0:
                    act.wait_ge(s_const, 3)
                if g >= 2:
                    act.wait_ge(s_rs, g - 1)
                nc.scalar.activation(sd[:, b], mv[:, b, :, 1], ACT.Sqrt, bias=eps_sb[:, 0:1]).then_inc(s_sd, 1)
                act.wait_ge(s_nb, g + 1)
                if g >= 2:
                    act.wait_ge(s_hlo, g - 1)
                for j in range(CPB):
                    nc.scalar.activation(h32[:, b, j], xg[:, g % XG, j], ACT.Relu, bias=nb_h[:, b, j:j + 1],
                                         scale=rs_h[:, b, j:j + 1]).then_inc(s_h, 1)

            def uT_out(k):
                act.wait_ge(s_uTps, k.t + 1)
                if due(k.t):
                    act.wait_ge(s_fin, k.t)
                nc.scalar.activation(uT[:, :, :].rearrange("p c q -> p (c q)"), ps_uT[:, 0:D], ACT.Copy
                                     ).then_inc(s_uT, 1)

            def exp_block(k, b):
                nc.scalar.activation(s32[:, k.par, b * BLOCK:(b + 1) * BLOCK], s32[:, k.par, b * BLOCK:(b + 1) * BLOCK],
                                     ACT.Exp, bias=negm[:, k.par:k.par + 1], scale=invc_x[:, k.par:k.par + 1],
                                     accum_out=psums[:, k.par, b:b + 1]).then_inc(s_exp, 1)

            def p_high(k, b):
                act.wait_ge(s_exp, k.t * NB + b + 1)
                u = b // BPU
                if u >= 2:
                    act.wait_ge(s_pT[u - 2], k.t * 16 + 16)
                elif due(k.t):
                    act.wait_ge(s_pT[u + 2], k.t * 16)
                at = b % BPU * BLOCK
                nc.scalar.activation(p_hl[:, u % 2, 0, at:at + BLOCK], s32[:, k.par, b * BLOCK:(b + 1) * BLOCK],
                                     ACT.Copy, scale=P_SCALE).then_inc(s_phi, 1)

            act.wait_ge(s_mps, 1)
            nc.scalar.activation(m_sb[:, :, :].rearrange("p c d -> p (c d)"), ps_fin[:, :], ACT.Copy, scale=SCALE
                                 ).then_inc(s_m, 1)
            for g in range(NB):
                h_apply(g)

            def step(prev, cur, nxt, nxt2, nxt3, finish=True, weigh=True, score=True, project=True):
                if weigh:
                    act.wait_ge(s_negm, cur.t * 2 + 2)
                    if due(cur.t - 1):
                        act.wait_ge(s_w, (cur.t - 1) * 2)
                    nc.scalar.activation(mass[:, cur.par, 1:3], gs_es[:, cur.par], ACT.Exp,
                                         bias=negm[:, cur.par:cur.par + 1]).then_inc(s_ge, 1)
                    exp_block(cur, 0)
                for b in range(NB):
                    if weigh:
                        if b + 1 < NB:
                            exp_block(cur, b + 1)
                        p_high(cur, b)
                    if b == 5 and finish:
                        uT_out(prev)

            schedule(act, step)

        @block.tensor
        def _(pe):
            def project(k):
                pe.wait_ge(s_mxq[k.par], k.half * 16 + 16)
                if due(k.t):
                    pe.wait_ge(s_qlo, k.t)
                for c in range(DC):
                    last = nc.tensor.matmul(ps_q[:, 0:D], mxT_q[:, k.par, c], m_sb[:, c], start=c == 0, stop=c == DC - 1)
                last.then_inc(s_q, 1)

            def side_scores(k):
                if due(k.t):
                    pe.wait_ge(s_gsc, k.t)
                for c in range(DC):
                    last = nc.tensor.matmul(ps_gs, mxT_q[:, k.par, c], wge[:, c], start=c == 0, stop=c == DC - 1)
                last.then_inc(s_gs, 1)

            def scores(k, b):
                n = k.t * NB + b
                if b == 0:
                    pe.wait_ge(s_qT[k.par], k.half * 16 + 16)
                if due(n - 1):
                    pe.wait_ge(s_mask, n - 1)
                first = True
                for q_half, h_half in ((1, 0), (0, 1), (0, 0)):
                    for c in range(DC):
                        last = nc.tensor.matmul(ps_scores[:, b % 2], qT[:, k.par, q_half * DC + c],
                                                hT[:, b * CPB:(b + 1) * CPB, h_half * DC + c, :],
                                                start=first, stop=q_half + h_half == 0 and c == DC - 1)
                        first = False
                last.then_inc(s_s, 1)

            def p_times_h(k, b):
                if b == 0 and due(k.t - 1):
                    pe.wait_ge(s_un, k.t - 1)
                u, at = b // BPU, b % BPU * CPB
                if b % BPU == 0:
                    pe.wait_ge(s_pT[u], k.t * 16 + 16)
                for j in range(CPB):
                    kc = b * CPB + j
                    nc.tensor.matmul(ps_u[:, k.par], pT[:, u, 0, at + j], h_rows[:, kc, :],
                                     start=kc == 0, stop=False)
                    last = nc.tensor.matmul(ps_u[:, k.par, 0:D], pT[:, u, 1, at + j], h_rows[:, kc, 0:D],
                                            start=False, stop=kc == NB * CPB - 1)
                last.then_inc(s_pv, 1)

            def u_transposes(k):
                pe.wait_ge(s_un, k.t + 1)
                if due(k.t):
                    pe.wait_ge(s_uT, k.t)
                for c in range(DC):
                    last = nc.tensor.transpose(ps_uT[:, c * P:(c + 1) * P], un[:, c * P:(c + 1) * P], ident32[:, :])
                last.then_inc(s_uTps, 1)

            def final(k):
                pe.wait_ge(s_mxf[k.par], k.half * 16 + 16)
                if due(k.t):
                    pe.wait_ge(s_res, (k.t - 1) * 5 + 2)
                for c in range(DC):
                    nc.tensor.matmul(ps_fin[:, D:2 * D], mxT_f[:, k.par, c], wev_sb[:, c], start=c == 0, stop=c == DC - 1)
                pe.wait_ge(s_uT, k.t + 1)
                for c in range(DC):
                    last = nc.tensor.matmul(ps_fin[:, 0:D], uT[:, c], wlv_sb[:, c], start=c == 0, stop=c == DC - 1)
                last.then_inc(s_fin, 1)

            def mean_rows(g):
                pe.wait_ge(s_hhi, g + 1)
                pe.wait_ge(s_hlo, g + 1)
                for j in range(CPB):
                    kc = g * CPB + j
                    last = nc.tensor.matmul(ps_u[0:1, 0], ones16[:, 0:1], h_rows[:, kc, :], start=kc == 0,
                                            stop=kc == NB * CPB - 1)
                if g == NB - 1:
                    last.then_inc(s_xbar, 1)

            pe.wait_ge(s_wqk, 32)
            for ic in range(DC):
                for c in range(DC):
                    last = nc.tensor.matmul(ps_fin[:, ic * D:(ic + 1) * D], wq_t[:, c, ic * P:(ic + 1) * P],
                                            wk_t[:, c], start=c == 0, stop=c == DC - 1)
            last.then_inc(s_mps, 1)
            pe.wait_ge(s_m, 1)
            project(Tile(0, 0))
            pe.wait_ge(s_ident, 1)
            pe.wait_ge(s_const, 2)
            for g in range(NB):
                mean_rows(g)
                if g == 3:
                    project(Tile(0, 1))
                if g >= 1:
                    pe.wait_ge(s_hT[(g - 1) % XG], 16 * ((g - 1) // XG + 1))
                    scores(Tile(0, 0), g - 1)
            pe.wait_ge(s_hT[(NB - 1) % XG], 16 * ((NB - 1) // XG + 1))
            scores(Tile(0, 0), NB - 1)
            pe.wait_ge(s_gev, 1)
            for c in range(DC):
                for hl in range(2):
                    last = nc.tensor.matmul(ps_small[:, c:c + 1], xbar_row[0:1, hl * D + c * P:hl * D + (c + 1) * P],
                                            ones32[0:1, 0:1], start=hl == 0, stop=hl == 1)
            last.then_inc(s_gstep, 1)
            pe.wait_ge(s_wg, 64)
            pe.wait_ge(s_gev, 2)
            for jc in range(DC):
                for c in range(DC):
                    last = nc.tensor.matmul(ps_small[:, 4 + jc:5 + jc], wgk_sb[:, c, jc * P:(jc + 1) * P],
                                            xbarT[:, c:c + 1], start=c == 0, stop=c == DC - 1)
            last.then_inc(s_gstep, 1)
            pe.wait_ge(s_gev, 3)
            for ic in range(DC):
                for c in range(DC):
                    last = nc.tensor.matmul(ps_small[:, 8 + ic:9 + ic], wgq_t[:, c, ic * P:(ic + 1) * P],
                                            gk_u[:, c:c + 1], start=c == 0, stop=c == DC - 1)
            last.then_inc(s_gstep, 1)
            pe.wait_ge(s_gev, 6)
            for c in range(DC):
                last = nc.tensor.matmul(ps_fin[:, 0:D], xbar_bc[:, c], wgv_sb[:, c], start=c == 0, stop=c == DC - 1)
            last.then_inc(s_gstep, 1)
            side_scores(Tile(0, 0))
            side_scores(Tile(0, 1))
            pe.wait_ge(s_gev, 7)

            def step(prev, cur, nxt, nxt2, nxt3, finish=True, weigh=True, score=True, project_=True):
                for b in range(NB):
                    if score:
                        scores(nxt, b)
                    if b < LAG and finish:
                        p_times_h(prev, b + NB - LAG)
                    if b >= LAG and weigh:
                        p_times_h(cur, b - LAG)
                    if b == 0 and project_:
                        project(nxt2)
                        side_scores(nxt2)
                    if b == 5 and finish:
                        u_transposes(prev)
                    if b == 6 and finish:
                        final(prev)

            def step_(*a, project=True, **k):
                step(*a, project_=project, **k)

            schedule(pe, step_)

        @block.vector
        def _(dve):
            def h_stats(g):
                b = g % 2
                dve.wait_ge(s_x[g % XG], 16 * (g // XG + 1))
                for j in range(CPB):
                    nc.vector.bn_stats(st6[:, b, j], xg[:, g % XG, j]).then_inc(s_bn, 1)
                for j in range(CPB):
                    dve.wait_ge(s_bn, CPB * g + j + 1)
                    nc.vector.bn_aggr(mv[:, b, j], st6[:, b, j]).then_inc(s_mv, 1)

            def h_scales(g):
                b = g % 2
                dve.wait_ge(s_sd, g + 1)
                nc.vector.reciprocal(rs[:, b], sd[:, b]).then_inc(s_rs, 1)
                dve.wait_ge(s_rs, g + 1)
                if g >= 2:
                    dve.wait_ge(s_h, CPB * (g - 1))
                nc.vector.tensor_scalar(rs_h[:, b], rs[:, b], H_SCALE, None, ALU.mult).then_inc(s_rsh, 1)
                dve.wait_ge(s_rsh, g + 1)
                dve.wait_ge(s_mv, CPB * (g + 1))
                nc.vector.scalar_tensor_tensor(nb_h[:, b], mv[:, b, :, 0], -1.0, rs_h[:, b], ALU.mult, ALU.mult
                                               ).then_inc(s_nb, 1)

            def h_high(g):
                dve.wait_ge(s_h, CPB * (g + 1))
                nc.vector.tensor_copy(h_rows[:, g * CPB:(g + 1) * CPB, 0:D], h32[:, g % 2]).then_inc(s_hhi, 1)

            def q_split(k):
                dve.wait_ge(s_q, k.t + 1)
                nc.vector.tensor_reduce(rmax[:, :], ps_q[:, 0:D], AX_X, ALU.max, apply_absolute_value=True
                                        ).then_inc(s_rowscale, 1)
                dve.wait_ge(s_rowscale, k.t * 4 + 1)
                nc.vector.tensor_scalar(rclamp[:, :], rmax[:, :], TINY, None, ALU.max).then_inc(s_rowscale, 1)
                dve.wait_ge(s_rowscale, k.t * 4 + 2)
                nc.vector.tensor_scalar(rpow[:, :].bitcast(I32), rclamp[:, :].bitcast(I32), 0x7F800000, None,
                                        ALU.bitwise_and).then_inc(s_rowscale, 1)
                dve.wait_ge(s_rowscale, k.t * 4 + 3)
                nc.vector.tensor_scalar(cinv[:, :], rpow[:, :], 1.0 / Q_TOP, None, ALU.mult).then_inc(s_rowscale, 1)
                nc.vector.tensor_scalar(invc[:, k.par:k.par + 1], rpow[:, :], 1.0 / (Q_TOP * H_SCALE), None, ALU.mult
                                        ).then_inc(s_invc, 1)
                dve.wait_ge(s_rowscale, k.t * 4 + 4)
                nc.vector.reciprocal(cq[:, :], cinv[:, :]).then_inc(s_cq, 1)
                dve.wait_ge(s_cq, k.t + 1)
                if due(k.t - 1):
                    dve.wait_ge(s_qT[k.par], k.half * 16)
                nc.vector.tensor_scalar(q_hl[:, k.par, 0], ps_q[:, 0:D], cq[:, 0:1], None, ALU.mult).then_inc(s_qhi, 1)
                if due(k.t - 1):
                    dve.wait_ge(s_bias, (k.t - 1) * MB)
                for n, sign in enumerate((1.0, -1.0)):
                    nc.vector.tensor_scalar(big[:, k.par, n:n + 1], cq[:, :], sign * MASKED * H_SCALE, None, ALU.mult
                                            ).then_inc(s_big, 1)
                dve.wait_ge(s_qhi, k.t + 1)
                nc.vector.scalar_tensor_tensor(q_hl[:, k.par, 1], ps_q[:, 0:D], cq[:, 0:1], q_hl[:, k.par, 0], ALU.mult, ALU.subtract
                                               ).then_inc(s_qlo, 1)

            def side_out(k):
                dve.wait_ge(s_gs, k.t + 1)
                if due(k.t - 1):
                    dve.wait_ge(s_ge, k.t - 1)
                nc.vector.tensor_copy(gs_es[:, k.par], ps_gs).then_inc(s_gsc, 1)

            def add_mask(k, b):
                n = k.t * NB + b
                if b % BPM == 0:
                    dve.wait_ge(s_bias, k.t * MB + b // BPM + 1)
                dve.wait_ge(s_s, n + 1)
                if due(k.t - 1):
                    dve.wait_ge(s_plo, (k.t - 2) * NB + b + 1)
                dve.sem_inc(s_mask_go, 1)
                nc.vector.tensor_tensor_reduce(
                    out=s32[:, k.par, b * BLOCK:(b + 1) * BLOCK], in0=ps_scores[:, b % 2],
                    in1=bias[:, b * BLOCK:(b + 1) * BLOCK], scale=1.0, scalar=-3.0e38, op0=ALU.add, op1=ALU.max,
                    accum_out=bmax[:, k.par, b:b + 1]).then_inc(s_mask, 1)

            def row_max(k):
                par = slice(k.par, k.par + 1)
                dve.wait_ge(s_mask, (k.t + 1) * NB)
                dve.wait_ge(s_gsc, k.t + 1)
                dve.wait_ge(s_invc, k.t + 1)
                nc.vector.reduce_max(mloc[:, :], bmax[:, k.par], AX_X).then_inc(s_mloc, 1)
                if due(k.t - 1):
                    dve.wait_ge(s_exp, (k.t - 1) * NB)
                nc.vector.tensor_copy(invc_x[:, par], invc[:, par]).then_inc(s_negm, 1)
                dve.wait_ge(s_mloc, k.t * 2 + 1)
                nc.vector.tensor_scalar(m1[:, :], mloc[:, :], invc[:, par], gs_es[:, k.par, 0:1], ALU.mult, ALU.max
                                        ).then_inc(s_mloc, 1)
                dve.wait_ge(s_mloc, k.t * 2 + 2)
                nc.vector.tensor_scalar(negm[:, par], m1[:, :], gs_es[:, k.par, 1:2], -1.0, ALU.max, ALU.mult
                                        ).then_inc(s_negm, 1)

            def p_low(k, b):
                dve.wait_ge(s_phi, k.t * NB + b + 1)
                u, at = b // BPU, b % BPU * BLOCK
                nc.vector.scalar_tensor_tensor(
                    p_hl[:, u % 2, 1, at:at + BLOCK], s32[:, k.par, b * BLOCK:(b + 1) * BLOCK], P_SCALE,
                    p_hl[:, u % 2, 0, at:at + BLOCK], ALU.mult, ALU.subtract).then_inc(s_plo, 1)

            def weights(k):
                dve.wait_ge(s_exp, (k.t + 1) * NB)
                dve.wait_ge(s_ge, k.t + 1)
                nc.vector.reduce_sum(mass[:, k.par, 0:1], psums[:, k.par], AX_X).then_inc(s_den, 1)
                dve.wait_ge(s_den, k.t * 3 + 1)
                nc.vector.reduce_sum(den[:, :], mass[:, k.par], AX_X).then_inc(s_den, 1)
                dve.wait_ge(s_den, k.t * 3 + 2)
                nc.vector.reciprocal(rden[:, :], den[:, :]).then_inc(s_den, 1)
                dve.wait_ge(s_den, k.t * 3 + 3)
                nc.vector.tensor_scalar(r_u[:, :], rden[:, :], 1.0 / (P_SCALE * H_SCALE), None, ALU.mult
                                        ).then_inc(s_w, 1)
                nc.vector.tensor_scalar(w3[:, :], mass[:, k.par], rden[:, 0:1], None, ALU.mult).then_inc(s_w, 1)

            def u_out(k):
                dve.wait_ge(s_w, k.t * 2 + 2)
                dve.wait_ge(s_pv, (k.t + 1) * NB)
                nc.vector.tensor_scalar(u1[:, :], ps_u[:, k.par, D:2 * D], r_u[:, 0:1], None, ALU.mult).then_inc(s_u1, 1)
                dve.wait_ge(s_u1, k.t + 1)
                if due(k.t):
                    dve.wait_ge(s_uTps, k.t)
                nc.vector.scalar_tensor_tensor(un[:, :], ps_u[:, k.par, 0:D], r_u[:, 0:1], u1[:, :], ALU.mult, ALU.add
                                               ).then_inc(s_un, 1)

            def combine(k):
                dve.wait_ge(s_fin, k.t + 1)
                nc.vector.tensor_tensor(e2[:, :], ps_fin[:, D:2 * D], bev_b[:, :], ALU.add).then_inc(s_res, 1)
                dve.wait_ge(s_res, k.t * 5 + 1)
                nc.vector.scalar_tensor_tensor(r1[:, :], e2[:, :], w3[:, 2:3], ps_fin[:, 0:D], ALU.mult, ALU.add
                                               ).then_inc(s_res, 1)
                dve.wait_ge(s_res, k.t * 5 + 2)
                nc.vector.scalar_tensor_tensor(r2[:, :], blv_b[:, :], w3[:, 0:1], r1[:, :], ALU.mult, ALU.add
                                               ).then_inc(s_res, 1)
                dve.wait_ge(s_res, k.t * 5 + 3)
                nc.vector.scalar_tensor_tensor(r3[:, :], gv_b[:, :], w3[:, 1:2], r2[:, :], ALU.mult, ALU.add
                                               ).then_inc(s_res, 1)
                dve.wait_ge(s_res, k.t * 5 + 4)
                dve.wait_ge(s_xm[k.par], k.half * 32 + 32)
                if due(k.t - 1):
                    dve.wait_ge(s_o, k.t - 1)
                nc.vector.tensor_tensor(rows_done[:, k.par], r3[:, :], xm[:, k.par, 1], ALU.max).then_inc(s_res, 1)

            for g in range(NB):
                h_stats(g)
                h_scales(g)
                if g == 1:
                    q_split(Tile(0, 0))
                if g == 5:
                    q_split(Tile(0, 1))
                h_high(g)
                if g >= 2:
                    add_mask(Tile(0, 0), g - 2)
            add_mask(Tile(0, 0), NB - 2)
            dve.wait_ge(s_xbar, 1)
            nc.vector.tensor_scalar(xbar_row[:, :], ps_u[0:1, 0], 1.0 / (N * H_SCALE), None, ALU.mult).then_inc(s_gev, 1)
            add_mask(Tile(0, 0), NB - 1)
            dve.wait_ge(s_gstep, 1)
            nc.vector.tensor_copy(xbarT[:, :], ps_small[:, 0:DC]).then_inc(s_gev, 1)
            dve.wait_ge(s_gstep, 2)
            nc.vector.tensor_copy(gk_u[:, :], ps_small[:, 4:4 + DC]).then_inc(s_gev, 1)
            dve.wait_ge(s_gstep, 3)
            dve.wait_ge(s_wg, 64)
            nc.vector.tensor_scalar(wge[:, :, 0], ps_small[:, 8:8 + DC], SCALE, None, ALU.mult).then_inc(s_gev, 1)
            dve.wait_ge(s_gev, 2)
            for c in range(DC):
                nc.vector.tensor_scalar(xbar_bc[:, c], ones32[:, :], xbarT[:, c:c + 1], None, ALU.mult
                                        ).then_inc(s_gev, 1)
            dve.wait_ge(s_gstep, 4)
            dve.wait_ge(s_bc, 48)
            nc.vector.tensor_tensor(gv_b[:, :], ps_fin[:, 0:D], bgv_b[:, :], ALU.add).then_inc(s_gev, 1)
            side_out(Tile(0, 0))
            side_out(Tile(0, 1))
            row_max(Tile(0, 0))

            def step(prev, cur, nxt, nxt2, nxt3, finish=True, weigh=True, score=True, project=True):
                if finish:
                    weights(prev)
                for b in range(NB):
                    if score:
                        add_mask(nxt, b)
                        if b == NB - 1:
                            row_max(nxt)
                    if b == LAG and finish:
                        u_out(prev)
                    if weigh:
                        p_low(cur, b)
                    if b == 1 and project:
                        q_split(nxt2)
                        side_out(nxt2)
                if finish:
                    combine(prev)

            schedule(dve, step)


def kernel(x, adj, L0_gnn_masked_x, L0_gnn_Wlq, L0_gnn_Wlk, L0_gnn_Wlv, L0_gnn_blv, L0_gnn_Wgq, L0_gnn_Wgk,
           L0_gnn_Wgv, L0_gnn_bgv, L0_gnn_Wes, L0_gnn_Wev, L0_gnn_bev):
    import numpy as np
    import concourse.bacc as bacc
    from concourse.bass_utils import run_bass_kernel_spmd as run

    mx = np.asarray(L0_gnn_masked_x)
    N, D = mx.shape
    arrays = {
        "x": np.asarray(x),
        "adj": np.asarray(adj),
        "mxT": mx.reshape(N // P, P, D // P, P).transpose(0, 3, 2, 1),
        "mx": mx,
        "WlqT": np.asarray(L0_gnn_Wlq).T,
        "WlkT": np.asarray(L0_gnn_Wlk).T,
        "Wlv": np.asarray(L0_gnn_Wlv),
        "blv": np.asarray(L0_gnn_blv),
        "WgqT": np.asarray(L0_gnn_Wgq).T,
        "Wgk": np.asarray(L0_gnn_Wgk),
        "Wgv": np.asarray(L0_gnn_Wgv),
        "bgv": np.asarray(L0_gnn_bgv),
        "Wes": np.asarray(L0_gnn_Wes),
        "Wev": np.asarray(L0_gnn_Wev),
        "bev": np.asarray(L0_gnn_bev),
    }
    arrays = {name: np.ascontiguousarray(a) for name, a in arrays.items()}
    nc = bacc.Bacc("TRN2", target_bir_lowering=False, num_devices=1)
    args = [nc.dram_tensor(name, a.shape, mybir.dt.from_np(a.dtype), kind="ExternalInput").ap()
            for name, a in arrays.items()]
    args.append(nc.dram_tensor("out", (N, D), F32, kind="ExternalOutput").ap())
    build(nc, *args)
    return run(nc, [arrays], core_ids=[0]).results[0]["out"]
```

```python
from contextlib import ExitStack

import concourse.bass as bass
from concourse import mybir

P = 128
F32, F16, U8, I32 = mybir.dt.float32, mybir.dt.float16, mybir.dt.uint8, mybir.dt.int32
ALU, ACT = mybir.AluOpType, mybir.ActivationFunctionType
AX_X = mybir.AxisListType.X

BLOCK = 512
CPB = BLOCK // P
H_SCALE = 2.0 ** 11
P_SCALE = 2.0 ** 15
Q_TOP = 2.0 ** 14
EPS = 1e-5
MASKED = 1e9
TINY = 1e-18
W_SCALE = 2.0 ** 14
V_SCALE = 2.0 ** 10


class Tile:

    def __init__(self, pair, offset):
        self.t = pair * 2 + offset
        self.par = offset % 2
        self.half = pair + offset // 2


def due(n):
    return not isinstance(n, int) or n > 0


def build(nc, x, adj, mxT, mx, WlqT, WlkT, Wlv, blv, WgqT, WgkT, Wgv, bgv, Wes, Wev, bev, out):
    N, D = x.shape
    T = N // P
    NB = N // BLOCK
    DC = D // P
    SCALE = float(D) ** -0.5
    MB = 4
    MW = N // MB
    BPM = MW // BLOCK
    BPU = 2
    NU = NB // BPU
    LAG = 4
    EARLY = 5
    V_FIRST = 3
    V_SPLIT = 5
    HURRIED = 3
    XG = 4

    x_groups = x.rearrange("(g j p) d -> g p j d", p=P, j=CPB)

    with ExitStack() as ctx:
        def sb(name, shape, dt=F32):
            return ctx.enter_context(nc.sbuf_tensor(name, shape, dt))

        def psum(name, shape, dt=F32):
            return ctx.enter_context(nc.psum_tensor(name, shape, dt))

        def sem(name):
            return ctx.enter_context(nc.semaphore(name))

        ps_scores = psum("ps_scores", [P, 2, BLOCK])
        ps_u = psum("ps_u", [P, 2, 2 * D])
        ps_pro = ps_u[:, 1]
        ps_q = psum("ps_q", [P, 2 * D])
        ps_gs = ps_q[:, D:D + 2]
        ps_v = psum("ps_v", [P, 2, 2 * D])
        ps_e = ps_v[:, 0, 0:D]
        ps_small = psum("ps_small", [P, 2 * D])

        hT = sb("hT", [P, N // P, 2 * DC, P], F16)
        v_rows = sb("v_rows", [P, N // P, 2 * D], F16)
        h_rows = v_rows
        mge = sb("mge", [P, DC, D + 2])
        m_sb = mge[:, :, 0:D]
        v_unscale = sb("v_unscale", [P, D])
        wlv_sb = sb("wlv_sb", [P, DC, D])
        wev_sb = sb("wev_sb", [P, DC, D])
        blv_b = sb("blv_b", [P, D])
        bev_b = sb("bev_b", [P, D])
        gv_b = sb("gv_b", [P, D])
        ones16 = sb("ones16", [P, 2], F16)
        ones32 = sb("ones32", [P, P])
        eps_sb = sb("eps_sb", [P, 1])

        shared = sb("shared", [P, XG * CPB * D])
        xg = shared[:, :].rearrange("p (g j d) -> p g j d", g=XG, j=CPB)
        shared2 = sb("shared2", [P, NU * BPU * BLOCK])
        h32 = shared2[:, 0:2 * CPB * D].rearrange("p (g j d) -> p g j d", g=2, j=CPB)
        st6 = sb("st6", [P, XG, CPB, 6])
        mv = sb("mv", [P, XG, CPB, 2])
        sd = sb("sd", [P, XG, CPB])
        rs = sb("rs", [P, XG, CPB])
        rs_h = sb("rs_h", [P, XG, CPB])
        nb_h = sb("nb_h", [P, XG, CPB])
        wq_t = sb("wq_t", [P, DC, D])
        wk_t = sb("wk_t", [P, DC, D])
        wgq_t = sb("wgq_t", [P, DC, D])
        wgk_t = sb("wgk_t", [P, DC, D])
        wgv_sb = sb("wgv_sb", [P, DC, D])
        bgv_b = sb("bgv_b", [P, D])
        xbarT = sb("xbarT", [P, DC])
        xbar_bc = sb("xbar_bc", [P, DC, P])
        g_sb = sb("g_sb", [P, DC, D])
        w_sq = sb("w_sq", [P, DC, D])
        w_norm = sb("w_norm", [P, D])
        w_inv = sb("w_inv", [P, D])
        w_hl = sb("w_hl", [P, 2, DC, D], F16)

        adj8 = sb("adj8", [P, 2, N], U8)
        mxT_q = sb("mxT_q", [P, 2, DC, P])
        mxT_f = sb("mxT_f", [P, 2, DC, P])
        xm = sb("xm", [P, 2, 2, D])
        s32 = sb("s32", [P, 2, N])
        qT = sb("qT", [P, 2, 2 * DC, P], F16)
        q_hl = sb("q_hl", [P, 2, 2, D], F16)
        invc = sb("invc", [P, 2])
        invc_x = sb("invc_x", [P, 2])
        big = sb("big", [P, 2, 2])
        gs_es = sb("gs_es", [P, 2, 2])
        bmax = sb("bmax", [P, 2, NB])
        negm = sb("negm", [P, 2])
        psums = sb("psums", [P, 2, NB])
        mass = sb("mass", [P, 2, 3])
        rows_done = sb("rows_done", [P, 2, D])
        o_sb = sb("o_sb", [P, 2, D])

        bias = sb("bias", [P, N])
        rmax = sb("rmax", [P, 1])
        rclamp = sb("rclamp", [P, 1])
        rpow = sb("rpow", [P, 1])
        cinv = sb("cinv", [P, 1])
        cq = sb("cq", [P, 1])
        mloc = sb("mloc", [P, 1])
        m1 = sb("m1", [P, 1])
        den = sb("den", [P, 1])
        rden = sb("rden", [P, 1])
        r_u = sb("r_u", [P, 1])
        w3 = sb("w3", [P, 3])
        u1 = sb("u1", [P, D])
        un = sb("un", [P, D])
        e2 = sb("e2", [P, D])
        ur = sb("ur", [P, D])
        r1 = sb("r1", [P, D])
        r2 = sb("r2", [P, D])
        r3 = sb("r3", [P, D])
        p_hl = shared2[:, :].bitcast(F16).rearrange("p (u a k) -> p u a k", u=NU, a=2)
        pT = shared[:, :].bitcast(F16).rearrange(
            "p (u a c q) -> p u a c q", u=NU, a=2, q=P)

        s_x = [sem(f"s_x{i}") for i in range(XG)]
        s_hT = [sem(f"s_hT{i}") for i in range(XG)]
        s_qT = [sem(f"s_qT{i}") for i in range(2)]
        s_pT = [sem(f"s_pT{i}") for i in range(NU)]
        s_wqk, s_wg, s_wgv, s_wlv, s_wev, s_bc = sem("s_wqk"), sem("s_wg"), sem("s_wgv"), sem("s_wlv"), sem("s_wev"), sem("s_bc")
        s_adj = [sem(f"s_adj{i}") for i in range(2)]
        s_mxq = [sem(f"s_mxq{i}") for i in range(2)]
        s_mxf = [sem(f"s_mxf{i}") for i in range(2)]
        s_xm = [sem(f"s_xm{i}") for i in range(2)]
        s_out = [sem(f"s_out{i}") for i in range(2)]
        s_const = sem("s_const")
        s_bn, s_mv, s_sd, s_rs, s_rsh, s_nb = (sem(n) for n in ("s_bn", "s_mv", "s_sd", "s_rs", "s_rsh", "s_nb"))
        s_h, s_hhi, s_hlo = sem("s_h"), sem("s_hhi"), sem("s_hlo")
        s_mps, s_m = sem("s_mps"), sem("s_m")
        s_wsq, s_wnps, s_wnorm, s_ws, s_whi, s_wlo = (
            sem(n) for n in ("s_wsq", "s_wnps", "s_wnorm", "s_ws", "s_whi", "s_wlo"))
        s_v, s_vhi, s_vlo = sem("s_v"), sem("s_vhi"), sem("s_vlo")
        s_xbar, s_gstep, s_gev = sem("s_xbar"), sem("s_gstep"), sem("s_gev")
        s_q, s_rowscale, s_cq, s_invc, s_big = sem("s_q"), sem("s_rowscale"), sem("s_cq"), sem("s_invc"), sem("s_big")
        s_qhi, s_qlo = sem("s_qhi"), sem("s_qlo")
        s_gs, s_gsc = sem("s_gs"), sem("s_gsc")
        s_bias, s_s, s_mask, s_mloc, s_negm = sem("s_bias"), sem("s_s"), sem("s_mask"), sem("s_mloc"), sem("s_negm")
        s_mask_go, s_bias_go, s_sp_go = sem("s_mask_go"), sem("s_bias_go"), sem("s_sp_go")
        s_exp, s_ge, s_phi, s_plo, s_pv = (sem(n) for n in ("s_exp", "s_ge", "s_phi", "s_plo", "s_pv"))
        s_den, s_w, s_e, s_e2, s_rest, s_u1, s_un, s_res, s_o = (
            sem(n) for n in ("s_den", "s_w", "s_e", "s_e2", "s_rest", "s_u1", "s_un", "s_res", "s_o"))

        block = ctx.enter_context(nc.Block())

        def schedule(eng, step):
            def tiles(pair, o):
                return [Tile(pair, o + k) for k in (-1, 0, 1, 2, 3)]

            step(*tiles(0, 0), finish=False, values=True)
            step(*tiles(0, 1))
            with eng.Fori(0, (T - 4) // 2) as j:
                step(*tiles(j, 2))
                step(*tiles(j, 3))
            step(*tiles(0, T - 2), project=False)
            step(*tiles(0, T - 1), project=False, score=False)
            step(*tiles(0, T), project=False, score=False, weigh=False)

        def v_steps(b):
            return range(b * CPB // 2, (b + 1) * CPB // 2)

        def carry(sp):
            sp.sem_inc(s_sp_go, 1)

        @block.sync
        def _(sp):
            def load_x(g):
                if g >= XG:
                    sp.wait_ge(s_h, CPB * (g - XG + 1))
                    sp.wait_ge(s_bn, CPB * (g - XG + 1))
                sp.dma_start(xg[:, g % XG], x_groups[g]).then_inc(s_x[g % XG], 16)

            def transpose_h(g):
                sp.wait_ge(s_hhi, g + 1)
                sp.wait_ge(s_hlo, g + 1)
                sp.dma_start_transpose(
                    hT[:, g * CPB:(g + 1) * CPB].rearrange("p k c q -> p (k c) q"),
                    h_rows[:, g * CPB:(g + 1) * CPB].rearrange("p k d -> p (k d)")).then_inc(s_hT[g % XG], 16)

            def transpose_q(k):
                sp.wait_ge(s_qlo, k.t + 1)
                carry(sp)
                if due(k.t - 1):
                    sp.wait_ge(s_s, (k.t - 1) * NB)
                    carry(sp)
                sp.dma_start_transpose(qT[:, k.par], q_hl[:, k.par].rearrange("p a d -> p (a d)")
                                       ).then_inc(s_qT[k.par], 16)

            def transpose_p(k, u):
                sp.wait_ge(s_plo, k.t * NB + (u + 1) * BPU)
                carry(sp)
                if due(k.t):
                    sp.wait_ge(s_pv, (k.t - 1) * NB + (u + 1) * BPU)
                    carry(sp)
                sp.dma_start_transpose(pT[:, u].rearrange("p a c q -> p (a c) q"),
                                       p_hl[:, u].rearrange("p a k -> p (a k)")).then_inc(s_pT[u], 16)

            def load_adj(k):
                if due(k.t - 1):
                    sp.wait_ge(s_bias, (k.t - 1) * MB)
                    carry(sp)
                sp.dma_start(adj8[:, k.par], adj[bass.ds(k.t * P, P), :]).then_inc(s_adj[k.par], 16)

            def load_mxT_q(k):
                if due(k.t - 1):
                    sp.wait_ge(s_q, k.t - 1)
                    carry(sp)
                    if isinstance(k.t, int) and k.t < 4:
                        sp.wait_ge(s_gs, k.t - 1)
                        carry(sp)
                sp.dma_start(mxT_q[:, k.par], mxT[bass.ds(k.t, 1)].rearrange("a p c q -> (a p) c q")
                             ).then_inc(s_mxq[k.par], 16)

            def load_mxT_f(k):
                if due(k.t - 1):
                    sp.wait_ge(s_e, k.t - 1)
                    carry(sp)
                sp.dma_start(mxT_f[:, k.par], mxT[bass.ds(k.t, 1)].rearrange("a p c q -> (a p) c q")
                             ).then_inc(s_mxf[k.par], 16)

            def load_rows(k):
                if due(k.t - 1):
                    sp.wait_ge(s_o, k.t - 1)
                    carry(sp)
                sp.dma_start(xm[:, k.par, 0], x[bass.ds(k.t * P, P), :]).then_inc(s_xm[k.par], 16)
                sp.dma_start(xm[:, k.par, 1], mx[bass.ds(k.t * P, P), :]).then_inc(s_xm[k.par], 16)

            def cols(w):
                return w.rearrange("(c p) d -> p c d", p=P)

            load_x(0)
            sp.dma_start(wq_t[:, :, :], cols(WlqT)).then_inc(s_wqk, 16)
            sp.dma_start(wk_t[:, :, :], cols(WlkT)).then_inc(s_wqk, 16)
            load_x(1)
            load_mxT_q(Tile(0, 0))
            load_x(2)
            load_adj(Tile(0, 0))
            load_x(3)
            sp.dma_start(wlv_sb[:, :, :], cols(Wlv)).then_inc(s_wlv, 16)
            load_mxT_q(Tile(0, 1))
            for dst, src in ((wgq_t, WgqT), (wgk_t, WgkT)):
                sp.dma_start(dst[:, :, :], cols(src)).then_inc(s_wg, 16)
            for g in range(NB):
                if g + XG < NB:
                    load_x(g + XG)
                if g == 7:
                    transpose_q(Tile(0, 1))
                if g == 1:
                    transpose_q(Tile(0, 0))
                transpose_h(g)
                if g == 2:
                    sp.dma_start(wgv_sb[:, :, :], cols(Wgv)).then_inc(s_wgv, 16)
                    with nc.allow_non_contiguous_dma(reason="a column of 256 words"):
                        sp.dma_start(mge[:, :, D + 1:D + 2], cols(Wes)).then_inc(s_wgv, 16)
                if g == 3:
                    load_adj(Tile(0, 1))
                if g == 5:
                    sp.dma_start(wev_sb[:, :, :], cols(Wev)).then_inc(s_wev, 16)
                    for dst, src in ((blv_b, blv), (bev_b, bev), (bgv_b, bgv)):
                        sp.dma_start(dst[:, :], src.partition_broadcast(P)).then_inc(s_bc, 16)
            load_adj(Tile(0, 2))
            load_mxT_q(Tile(0, 2))

            def step(prev, cur, nxt, nxt2, nxt3, finish=True, weigh=True, project=True):
                if weigh:
                    load_mxT_f(cur)
                    transpose_p(cur, 0)
                    load_rows(cur)
                if project:
                    transpose_q(nxt2)
                if weigh:
                    transpose_p(cur, 1)
                if project and (not isinstance(nxt3.t, int) or nxt3.t < T):
                    load_mxT_q(nxt3)
                    load_adj(nxt3)
                if weigh:
                    transpose_p(cur, 2)
                    transpose_p(cur, 3)
                if finish:
                    sp.wait_ge(s_o, prev.t + 1)
                    carry(sp)
                    sp.dma_start(out[bass.ds(prev.t * P, P), :], o_sb[:, prev.par]).then_inc(s_out[prev.par], 16)

            step(*[Tile(0, k) for k in (-1, 0, 1, 2, 3)], finish=False)
            step(*[Tile(0, k) for k in (0, 1, 2, 3, 4)])
            with sp.Fori(0, (T - 6) // 2) as j:
                step(*[Tile(j, 2 + k) for k in (-1, 0, 1, 2, 3)])
                step(*[Tile(j, 3 + k) for k in (-1, 0, 1, 2, 3)])
            for i in range(T - 4, T + 1):
                step(*[Tile(0, i + k) for k in (-1, 0, 1, 2, 3)], weigh=i < T, project=i + 2 < T)
            for par in range(2):
                sp.wait_ge(s_out[par], 16 * (T // 2))

        @block.gpsimd
        def _(pool):
            nc.gpsimd.memset(ones16[:, :], 1.0).then_inc(s_const, 1)
            nc.gpsimd.memset(ones32[:, :], 1.0).then_inc(s_const, 1)
            nc.gpsimd.memset(eps_sb[:, :], EPS).then_inc(s_const, 1)

            def h_low(g):
                pool.wait_ge(s_hhi, g + 1)
                nc.gpsimd.tensor_tensor(h_rows[:, g * CPB:(g + 1) * CPB, D:2 * D], h32[:, g % 2],
                                        h_rows[:, g * CPB:(g + 1) * CPB, 0:D], ALU.subtract).then_inc(s_hlo, 1)

            def mask_bias(k, b):
                if b == 0:
                    pool.wait_ge(s_adj[k.par], k.half * 16 + 16)
                    pool.wait_ge(s_big, k.t * 2 + 2)
                if due(k.t):
                    pool.wait_ge(s_mask, (k.t - 1) * NB + (b + 1) * BPM)
                pool.sem_inc(s_bias_go, 1)
                nc.gpsimd.tensor_scalar(bias[:, b * MW:(b + 1) * MW], adj8[:, k.par, b * MW:(b + 1) * MW],
                                        big[:, k.par, 0:1], big[:, k.par, 1:2], ALU.mult, ALU.add
                                        ).then_inc(s_bias, 1)

            def add_x(k):
                pool.wait_ge(s_res, k.t * 3 + 3)
                if due(k.t - 1):
                    pool.wait_ge(s_out[k.par], k.half * 16)
                pool.wait_ge(s_xm[k.par], k.half * 32 + 32)
                nc.gpsimd.tensor_tensor(o_sb[:, k.par], rows_done[:, k.par], xm[:, k.par, 0], ALU.add
                                        ).then_inc(s_o, 1)

            for g in range(NB):
                h_low(g)
                if 2 <= g < 2 + MB:
                    mask_bias(Tile(0, 0), g - 2)
            for b in range(MB):
                mask_bias(Tile(0, 1), b)

            def step(prev, cur, nxt, nxt2, nxt3, finish=True, weigh=True, score=True, project=True,
                     values=False):
                if project:
                    for b in range(MB - 1):
                        mask_bias(nxt2, b)
                if finish:
                    add_x(prev)
                if project:
                    mask_bias(nxt2, MB - 1)

            schedule(pool, step)

        @block.scalar
        def _(act):
            def h_deviation(g):
                b = g % XG
                act.wait_ge(s_mv, CPB * (g + 1))
                if g == 0:
                    act.wait_ge(s_const, 3)
                if g >= XG:
                    act.wait_ge(s_rs, g - XG + 1)
                nc.scalar.activation(sd[:, b], mv[:, b, :, 1], ACT.Sqrt, bias=eps_sb[:, 0:1]).then_inc(s_sd, 1)

            def h_apply(g):
                b = g % XG
                act.wait_ge(s_nb, g + 1)
                if g >= 2:
                    act.wait_ge(s_hlo, g - 1)
                for j in range(CPB):
                    nc.scalar.activation(h32[:, g % 2, j], xg[:, b, j], ACT.Relu, bias=nb_h[:, b, j:j + 1],
                                         scale=rs_h[:, b, j:j + 1]).then_inc(s_h, 1)

            def v_high(n):
                act.wait_ge(s_v, n + 1)
                nc.scalar.activation(v_rows[:, 2 * n:2 * n + 2, 0:D],
                                     ps_v[:, n % 2].rearrange("p (k d) -> p k d", k=2), ACT.Copy,
                                     scale=V_SCALE / (H_SCALE * W_SCALE)).then_inc(s_vhi, 1)

            def h_high(g):
                act.wait_ge(s_h, CPB * (g + 1))
                nc.scalar.activation(h_rows[:, g * CPB:(g + 1) * CPB, 0:D], h32[:, g % 2], ACT.Copy).then_inc(s_hhi, 1)

            def exp_block(k, b):
                nc.scalar.activation(s32[:, k.par, b * BLOCK:(b + 1) * BLOCK], s32[:, k.par, b * BLOCK:(b + 1) * BLOCK],
                                     ACT.Exp, bias=negm[:, k.par:k.par + 1], scale=invc_x[:, k.par:k.par + 1],
                                     accum_out=psums[:, k.par, b:b + 1]).then_inc(s_exp, 1)

            def p_high(k, b):
                act.wait_ge(s_exp, k.t * NB + b + 1)
                u = b // BPU
                if due(k.t):
                    act.wait_ge(s_pT[u], k.t * 16)
                at = b % BPU * BLOCK
                nc.scalar.activation(p_hl[:, u, 0, at:at + BLOCK], s32[:, k.par, b * BLOCK:(b + 1) * BLOCK],
                                     ACT.Copy, scale=P_SCALE).then_inc(s_phi, 1)

            h_deviation(0)
            for g in range(NB):
                if HURRIED < g < NB - 1:
                    h_deviation(g + 1)
                h_apply(g)
                if g <= HURRIED:
                    h_deviation(g + 1)
                h_high(g)
                if g == 0:
                    act.wait_ge(s_mps, 1)
                    nc.scalar.activation(m_sb, ps_pro.rearrange("p (c d) -> p c d", c=DC), ACT.Copy,
                                         scale=SCALE).then_inc(s_m, 1)
                if g == 1:
                    act.wait_ge(s_wlv, 16)
                    nc.scalar.activation(w_sq[:, :, :], wlv_sb[:, :, :], ACT.Square).then_inc(s_wsq, 1)
                if g == 2:
                    act.wait_ge(s_wnorm, 1)
                    nc.scalar.activation(w_norm[:, :], w_sq[:, 0], ACT.Sqrt).then_inc(s_wnorm, 1)
                if g == 3:
                    act.wait_ge(s_ws, DC)
                    nc.scalar.activation(w_hl[:, 0], w_sq[:, :, :], ACT.Copy, scale=W_SCALE / 2).then_inc(s_whi, 1)
                if g >= V_SPLIT:
                    for n in v_steps(g - V_SPLIT):
                        v_high(n)
                if g == 3:
                    act.wait_ge(s_mps, 2)
                    nc.scalar.activation(g_sb[:, :, :].rearrange("p c d -> p (c d)"), ps_pro, ACT.Copy,
                                         scale=SCALE).then_inc(s_m, 1)

            for b in range(NB - V_SPLIT, EARLY):
                for n in v_steps(b):
                    v_high(n)

            def step(prev, cur, nxt, nxt2, nxt3, finish=True, weigh=True, score=True, project=True,
                     values=False):
                if weigh:
                    act.wait_ge(s_negm, cur.t * 2 + 2)
                    if due(cur.t - 1):
                        act.wait_ge(s_w, (cur.t - 1) * 2)
                    nc.scalar.activation(mass[:, cur.par, 1:3], gs_es[:, cur.par], ACT.Exp,
                                         bias=negm[:, cur.par:cur.par + 1]).then_inc(s_ge, 1)
                    exp_block(cur, 0)
                for b in range(NB):
                    if weigh:
                        if b + 1 < NB:
                            exp_block(cur, b + 1)
                        p_high(cur, b)
                    if values and EARLY + b < NB:
                        for n in v_steps(EARLY + b):
                            v_high(n)

            schedule(act, step)

        @block.tensor
        def _(pe):
            def project(k, cols=D + 2):
                pe.wait_ge(s_mxq[k.par], k.half * 16 + 16)
                if due(k.t):
                    pe.wait_ge(s_qlo, k.t)
                if cols > D:
                    pe.wait_ge(s_gsc, k.t)
                for c in range(DC):
                    last = nc.tensor.matmul(ps_q[:, 0:cols], mxT_q[:, k.par, c], mge[:, c, 0:cols], start=c == 0,
                                            stop=c == DC - 1)
                last.then_inc(s_q, 1)

            def side_scores(k):
                pe.wait_ge(s_mxq[k.par], 16)
                pe.wait_ge(s_qlo, 2)
                if due(k.t):
                    pe.wait_ge(s_gsc, k.t)
                for c in range(DC):
                    last = nc.tensor.matmul(ps_gs, mxT_q[:, k.par, c], mge[:, c, D:D + 2], start=c == 0,
                                            stop=c == DC - 1)
                last.then_inc(s_gs, 1)

            def scores(k, b):
                n = k.t * NB + b
                if b == 0:
                    pe.wait_ge(s_qT[k.par], k.half * 16 + 16)
                if due(n - 1):
                    pe.wait_ge(s_mask, n - 1)
                first = True
                for q_half, h_half in ((1, 0), (0, 1), (0, 0)):
                    for c in range(DC):
                        last = nc.tensor.matmul(ps_scores[:, b % 2], qT[:, k.par, q_half * DC + c],
                                                hT[:, b * CPB:(b + 1) * CPB, h_half * DC + c, :],
                                                start=first, stop=q_half + h_half == 0 and c == DC - 1)
                        first = False
                last.then_inc(s_s, 1)

            def p_times_v(k, b):
                if b == 0 and due(k.t - 1):
                    pe.wait_ge(s_un, k.t - 1)
                u, at = b // BPU, b % BPU * CPB
                if b % BPU == 0:
                    pe.wait_ge(s_pT[u], k.t * 16 + 16)
                if b == 0 and isinstance(k.t, int) and k.t == 1:
                    pe.wait_ge(s_gev, 5)
                if isinstance(k.t, int) and k.t == 0:
                    pe.wait_ge(s_vlo, (b + 1) * CPB // 2)
                for j in range(CPB):
                    kc = b * CPB + j
                    nc.tensor.matmul(ps_u[:, k.par], pT[:, u, 0, at + j], v_rows[:, kc, :],
                                     start=kc == 0, stop=False)
                    last = nc.tensor.matmul(ps_u[:, k.par, 0:D], pT[:, u, 1, at + j], v_rows[:, kc, 0:D],
                                            start=False, stop=kc == NB * CPB - 1)
                last.then_inc(s_pv, 1)

            def es_values(k):
                pe.wait_ge(s_mxf[k.par], k.half * 16 + 16)
                if isinstance(k.t, int) and k.t == 0:
                    pe.wait_ge(s_wev, 16)
                    pe.wait_ge(s_vlo, N // P // 2)
                if due(k.t):
                    pe.wait_ge(s_e2, k.t)
                for c in range(DC):
                    last = nc.tensor.matmul(ps_e, mxT_f[:, k.par, c], wev_sb[:, c], start=c == 0, stop=c == DC - 1)
                last.then_inc(s_e, 1)

            def v_product(n):
                if n == 0:
                    pe.wait_ge(s_wlo, 1)
                if n >= 2:
                    pe.wait_ge(s_vlo, n - 1)
                for j in range(2):
                    first = True
                    for h_half, w_half in ((1, 0), (0, 1), (0, 0)):
                        for c in range(DC):
                            last = nc.tensor.matmul(ps_v[:, n % 2, j * D:(j + 1) * D], hT[:, 2 * n + j, h_half * DC + c],
                                                    w_hl[:, w_half, c], start=first,
                                                    stop=h_half + w_half == 0 and c == DC - 1)
                            first = False
                last.then_inc(s_v, 1)

            def mean_columns(g):
                pe.wait_ge(s_hhi, g + 1)
                pe.wait_ge(s_hlo, g + 1)
                for kc in range(g * CPB, (g + 1) * CPB):
                    for c in range(DC):
                        for hl in range(2):
                            at = hl * D + c * P
                            last = nc.tensor.matmul(ps_u[:, 0, c:c + 1], h_rows[:, kc, at:at + P], ones16[:, 0:1],
                                                    start=kc + c + hl == 0, stop=kc == NB * CPB - 1 and hl == 1,
                                                    skip_group_check=True)
                if g == NB - 1:
                    last.then_inc(s_xbar, 1)

            def weight_product(out_bank, left, right):
                for ic in range(DC):
                    for c in range(DC):
                        last = nc.tensor.matmul(out_bank[:, ic * D:(ic + 1) * D], left[:, c, ic * P:(ic + 1) * P],
                                                right[:, c], start=c == 0, stop=c == DC - 1)
                last.then_inc(s_mps, 1)

            pe.wait_ge(s_wqk, 32)
            weight_product(ps_pro, wq_t, wk_t)
            pe.wait_ge(s_const, 2)
            for g in range(NB):
                if g == 0:
                    pe.wait_ge(s_m, 1)
                    project(Tile(0, 0), D)
                else:
                    mean_columns(g - 1)
                if g == 2:
                    project(Tile(0, 1), D)
                if g == 1:
                    pe.wait_ge(s_wsq, 1)
                    for c in range(DC):
                        last = nc.tensor.matmul(ps_small[:, D:2 * D], ones32[:, :], w_sq[:, c], start=c == 0,
                                                stop=c == DC - 1)
                    last.then_inc(s_wnps, 1)
                    pe.wait_ge(s_wg, 32)
                    weight_product(ps_pro, wgk_t, wgq_t)
                if 1 <= g < NB - 1:
                    pe.wait_ge(s_hT[(g - 1) % XG], 16 * ((g - 1) // XG + 1))
                    scores(Tile(0, 0), g - 1)
                if g >= V_FIRST and g - V_FIRST < EARLY:
                    for n in v_steps(g - V_FIRST):
                        v_product(n)
            mean_columns(NB - 1)
            pe.wait_ge(s_hT[(NB - 2) % XG], 16 * ((NB - 2) // XG + 1))
            scores(Tile(0, 0), NB - 2)
            pe.wait_ge(s_gev, 1)
            pe.wait_ge(s_m, 2)
            for ic in range(DC):
                for c in range(DC):
                    last = nc.tensor.matmul(ps_small[:, 8 + ic:9 + ic], g_sb[:, c, ic * P:(ic + 1) * P],
                                            xbarT[:, c:c + 1], start=c == 0, stop=c == DC - 1)
            last.then_inc(s_gstep, 1)
            pe.wait_ge(s_hT[(NB - 1) % XG], 16 * ((NB - 1) // XG + 1))
            scores(Tile(0, 0), NB - 1)
            pe.wait_ge(s_gev, 2)
            pe.wait_ge(s_wgv, 32)
            side_scores(Tile(0, 0))

            def step(prev, cur, nxt, nxt2, nxt3, finish=True, weigh=True, score=True, project_=True,
                     values=False):
                for b in range(NB):
                    if score:
                        scores(nxt, b)
                    if values and b == 0:
                        side_scores(Tile(0, 1))
                    if b < LAG and finish:
                        p_times_v(prev, b + NB - LAG)
                    if b == LAG and weigh and not score:
                        es_values(cur)
                    if b >= LAG and weigh:
                        p_times_v(cur, b - LAG)
                    if values and EARLY + b < NB:
                        for n in v_steps(EARLY + b):
                            v_product(n)
                    if values and b == 0:
                        pe.wait_ge(s_gev, 4)
                        for c in range(DC):
                            last = nc.tensor.matmul(ps_pro[:, 0:D], xbar_bc[:, c], wgv_sb[:, c], start=c == 0,
                                                    stop=c == DC - 1)
                        last.then_inc(s_gstep, 1)
                    if b == 0 and project_:
                        project(nxt2)
                    if b == 6 and weigh and score:
                        es_values(cur)

            def step_(*a, project=True, **k):
                step(*a, project_=project, **k)

            schedule(pe, step_)

        @block.vector
        def _(dve):
            def h_stats(g):
                b = g % XG
                dve.wait_ge(s_x[b], 16 * (g // XG + 1))
                for j in range(CPB):
                    nc.vector.bn_stats(st6[:, b, j], xg[:, b, j]).then_inc(s_bn, 1)
                for j in range(CPB):
                    dve.wait_ge(s_bn, CPB * g + j + 1)
                    nc.vector.bn_aggr(mv[:, b, j], st6[:, b, j]).then_inc(s_mv, 1)

            def h_scales(g):
                b = g % XG
                dve.wait_ge(s_sd, g + 1)
                nc.vector.reciprocal(rs[:, b], sd[:, b]).then_inc(s_rs, 1)
                dve.wait_ge(s_rs, g + 1)
                if g >= XG:
                    dve.wait_ge(s_h, CPB * (g - XG + 1))
                nc.vector.tensor_scalar(rs_h[:, b], rs[:, b], H_SCALE, None, ALU.mult).then_inc(s_rsh, 1)
                dve.wait_ge(s_rsh, g + 1)
                dve.wait_ge(s_mv, CPB * (g + 1))
                nc.vector.scalar_tensor_tensor(nb_h[:, b], mv[:, b, :, 0], -1.0, rs_h[:, b], ALU.mult, ALU.mult
                                               ).then_inc(s_nb, 1)

            def q_split(k):
                dve.wait_ge(s_q, k.t + 1)
                nc.vector.tensor_reduce(rmax[:, :], ps_q[:, 0:D], AX_X, ALU.max, apply_absolute_value=True
                                        ).then_inc(s_rowscale, 1)
                dve.wait_ge(s_rowscale, k.t * 4 + 1)
                nc.vector.tensor_scalar(rclamp[:, :], rmax[:, :], TINY, None, ALU.max).then_inc(s_rowscale, 1)
                dve.wait_ge(s_rowscale, k.t * 4 + 2)
                nc.vector.tensor_scalar(rpow[:, :].bitcast(I32), rclamp[:, :].bitcast(I32), 0x7F800000, None,
                                        ALU.bitwise_and).then_inc(s_rowscale, 1)
                dve.wait_ge(s_rowscale, k.t * 4 + 3)
                nc.vector.tensor_scalar(cinv[:, :], rpow[:, :], 1.0 / Q_TOP, None, ALU.mult).then_inc(s_rowscale, 1)
                nc.vector.tensor_scalar(invc[:, k.par:k.par + 1], rpow[:, :], 1.0 / (Q_TOP * H_SCALE), None, ALU.mult
                                        ).then_inc(s_invc, 1)
                dve.wait_ge(s_rowscale, k.t * 4 + 4)
                nc.vector.reciprocal(cq[:, :], cinv[:, :]).then_inc(s_cq, 1)
                dve.wait_ge(s_cq, k.t + 1)
                if due(k.t - 1):
                    dve.wait_ge(s_qT[k.par], k.half * 16)
                nc.vector.tensor_scalar(q_hl[:, k.par, 0], ps_q[:, 0:D], cq[:, 0:1], None, ALU.mult).then_inc(s_qhi, 1)
                if due(k.t - 1):
                    dve.wait_ge(s_bias, (k.t - 1) * MB)
                for n, sign in enumerate((1.0, -1.0)):
                    nc.vector.tensor_scalar(big[:, k.par, n:n + 1], cq[:, :], sign * MASKED * H_SCALE, None, ALU.mult
                                            ).then_inc(s_big, 1)
                dve.wait_ge(s_qhi, k.t + 1)
                nc.vector.scalar_tensor_tensor(q_hl[:, k.par, 1], ps_q[:, 0:D], cq[:, 0:1], q_hl[:, k.par, 0], ALU.mult, ALU.subtract
                                               ).then_inc(s_qlo, 1)

            def side_out(k):
                if isinstance(k.t, int) and k.t < 2:
                    dve.wait_ge(s_gs, k.t + 1)
                else:
                    dve.wait_ge(s_q, k.t + 1)
                if due(k.t - 1):
                    dve.wait_ge(s_ge, k.t - 1)
                nc.vector.tensor_copy(gs_es[:, k.par], ps_gs).then_inc(s_gsc, 1)

            def add_mask(k, b):
                n = k.t * NB + b
                if b % BPM == 0:
                    dve.wait_ge(s_bias, k.t * MB + b // BPM + 1)
                dve.wait_ge(s_s, n + 1)
                if due(k.t - 1):
                    dve.wait_ge(s_plo, (k.t - 2) * NB + b + 1)
                dve.sem_inc(s_mask_go, 1)
                nc.vector.tensor_tensor_reduce(
                    out=s32[:, k.par, b * BLOCK:(b + 1) * BLOCK], in0=ps_scores[:, b % 2],
                    in1=bias[:, b * BLOCK:(b + 1) * BLOCK], scale=1.0, scalar=-3.0e38, op0=ALU.add, op1=ALU.max,
                    accum_out=bmax[:, k.par, b:b + 1]).then_inc(s_mask, 1)

            def row_max(k):
                par = slice(k.par, k.par + 1)
                dve.wait_ge(s_mask, (k.t + 1) * NB)
                dve.wait_ge(s_gsc, k.t + 1)
                dve.wait_ge(s_invc, k.t + 1)
                nc.vector.reduce_max(mloc[:, :], bmax[:, k.par], AX_X).then_inc(s_mloc, 1)
                if due(k.t - 1):
                    dve.wait_ge(s_exp, (k.t - 1) * NB)
                nc.vector.tensor_copy(invc_x[:, par], invc[:, par]).then_inc(s_negm, 1)
                dve.wait_ge(s_mloc, k.t * 2 + 1)
                nc.vector.tensor_scalar(m1[:, :], mloc[:, :], invc[:, par], gs_es[:, k.par, 0:1], ALU.mult, ALU.max
                                        ).then_inc(s_mloc, 1)
                dve.wait_ge(s_mloc, k.t * 2 + 2)
                nc.vector.tensor_scalar(negm[:, par], m1[:, :], gs_es[:, k.par, 1:2], -1.0, ALU.max, ALU.mult
                                        ).then_inc(s_negm, 1)

            def p_low(k, b):
                dve.wait_ge(s_phi, k.t * NB + b + 1)
                u, at = b // BPU, b % BPU * BLOCK
                nc.vector.scalar_tensor_tensor(
                    p_hl[:, u, 1, at:at + BLOCK], s32[:, k.par, b * BLOCK:(b + 1) * BLOCK], P_SCALE,
                    p_hl[:, u, 0, at:at + BLOCK], ALU.mult, ALU.subtract).then_inc(s_plo, 1)

            def weights(k):
                dve.wait_ge(s_exp, (k.t + 1) * NB)
                dve.wait_ge(s_ge, k.t + 1)
                nc.vector.reduce_sum(mass[:, k.par, 0:1], psums[:, k.par], AX_X).then_inc(s_den, 1)
                dve.wait_ge(s_den, k.t * 3 + 1)
                nc.vector.reduce_sum(den[:, :], mass[:, k.par], AX_X).then_inc(s_den, 1)
                dve.wait_ge(s_den, k.t * 3 + 2)
                nc.vector.reciprocal(rden[:, :], den[:, :]).then_inc(s_den, 1)
                dve.wait_ge(s_den, k.t * 3 + 3)
                nc.vector.tensor_scalar(r_u[:, :], rden[:, :], 1.0 / (P_SCALE * V_SCALE), None, ALU.mult
                                        ).then_inc(s_w, 1)
                nc.vector.tensor_scalar(w3[:, :], mass[:, k.par], rden[:, 0:1], None, ALU.mult).then_inc(s_w, 1)

            def combine_rest(k):
                dve.wait_ge(s_w, k.t * 2 + 2)
                dve.wait_ge(s_e, k.t + 1)
                nc.vector.tensor_tensor(e2[:, :], ps_e, bev_b[:, :], ALU.add).then_inc(s_e2, 1)
                if due(k.t):
                    dve.wait_ge(s_res, k.t * 3)
                nc.vector.tensor_scalar(r1[:, :], blv_b[:, :], w3[:, 0:1], None, ALU.mult).then_inc(s_rest, 1)
                dve.wait_ge(s_e2, k.t + 1)
                dve.wait_ge(s_rest, k.t * 3 + 1)
                nc.vector.scalar_tensor_tensor(r2[:, :], e2[:, :], w3[:, 2:3], r1[:, :], ALU.mult, ALU.add
                                               ).then_inc(s_rest, 1)
                dve.wait_ge(s_rest, k.t * 3 + 2)
                nc.vector.scalar_tensor_tensor(r3[:, :], gv_b[:, :], w3[:, 1:2], r2[:, :], ALU.mult, ALU.add
                                               ).then_inc(s_rest, 1)

            def combine(k):
                dve.wait_ge(s_pv, (k.t + 1) * NB)
                nc.vector.tensor_scalar(u1[:, :], ps_u[:, k.par, D:2 * D], r_u[:, 0:1], None, ALU.mult).then_inc(s_u1, 1)
                dve.wait_ge(s_u1, k.t + 1)
                nc.vector.scalar_tensor_tensor(un[:, :], ps_u[:, k.par, 0:D], r_u[:, 0:1], u1[:, :], ALU.mult, ALU.add
                                               ).then_inc(s_un, 1)
                dve.wait_ge(s_un, k.t + 1)
                nc.vector.tensor_tensor(ur[:, :], un[:, :], v_unscale[:, :], ALU.mult).then_inc(s_res, 1)
                dve.wait_ge(s_res, k.t * 3 + 1)
                dve.wait_ge(s_rest, k.t * 3 + 3)
                nc.vector.tensor_tensor(u1[:, :], ur[:, :], r3[:, :], ALU.add).then_inc(s_res, 1)
                dve.wait_ge(s_res, k.t * 3 + 2)
                dve.wait_ge(s_xm[k.par], k.half * 32 + 32)
                if due(k.t - 1):
                    dve.wait_ge(s_o, k.t - 1)
                nc.vector.tensor_tensor(rows_done[:, k.par], u1[:, :], xm[:, k.par, 1], ALU.max).then_inc(s_res, 1)

            def v_low(n):
                dve.wait_ge(s_vhi, n + 1)
                nc.vector.scalar_tensor_tensor(
                    v_rows[:, 2 * n:2 * n + 2, D:2 * D], ps_v[:, n % 2].rearrange("p (k d) -> p k d", k=2),
                    V_SCALE / (H_SCALE * W_SCALE), v_rows[:, 2 * n:2 * n + 2, 0:D], ALU.mult, ALU.subtract
                    ).then_inc(s_vlo, 1)

            h_stats(0)
            h_scales(0)
            h_stats(1)
            for g in range(NB):
                if g + 1 < NB:
                    h_scales(g + 1)
                if g == 1:
                    q_split(Tile(0, 0))
                if g + 2 < NB:
                    h_stats(g + 2)
                if g == 1:
                    dve.wait_ge(s_wnps, 1)
                    nc.vector.tensor_scalar(w_sq[:, 0], ps_small[:, D:2 * D], TINY * TINY, None, ALU.max
                                            ).then_inc(s_wnorm, 1)
                if g == 2:
                    dve.wait_ge(s_wnorm, 2)
                    nc.vector.tensor_scalar(v_unscale[:, :].bitcast(I32), w_norm[:, :].bitcast(I32), 0x7F800000, None,
                                            ALU.bitwise_and).then_inc(s_wnorm, 1)
                    nc.vector.tensor_scalar(w_inv[:, :].bitcast(I32), w_norm[:, :].bitcast(I32), 0x7F800000, 0x7F800000,
                                            ALU.bitwise_and, ALU.bitwise_xor).then_inc(s_wnorm, 1)
                    dve.wait_ge(s_wnorm, 4)
                    for c in range(DC):
                        nc.vector.tensor_tensor(w_sq[:, c], wlv_sb[:, c], w_inv[:, :], ALU.mult).then_inc(s_ws, 1)
                if g == 3:
                    dve.wait_ge(s_whi, 1)
                    nc.vector.scalar_tensor_tensor(w_hl[:, 1], w_sq[:, :, :], W_SCALE / 2, w_hl[:, 0], ALU.mult, ALU.subtract
                                                   ).then_inc(s_wlo, 1)
                if g == 6:
                    q_split(Tile(0, 1))
                if g >= 3:
                    add_mask(Tile(0, 0), g - 3)
                if g >= V_SPLIT:
                    for n in v_steps(g - V_SPLIT):
                        v_low(n)
            for b in range(NB - V_SPLIT, EARLY):
                for n in v_steps(b):
                    v_low(n)
            dve.wait_ge(s_xbar, 1)
            nc.vector.tensor_scalar(xbarT[:, :], ps_u[:, 0, 0:DC], 1.0 / (N * H_SCALE), None, ALU.mult).then_inc(s_gev, 1)
            add_mask(Tile(0, 0), NB - 3)
            add_mask(Tile(0, 0), NB - 2)
            dve.wait_ge(s_gstep, 1)
            nc.vector.tensor_copy(mge[:, :, D:D + 1], ps_small[:, 8:8 + DC].rearrange("p (c a) -> p c a", a=1)).then_inc(s_gev, 1)
            add_mask(Tile(0, 0), NB - 1)
            side_out(Tile(0, 0))
            row_max(Tile(0, 0))

            def step(prev, cur, nxt, nxt2, nxt3, finish=True, weigh=True, score=True, project=True,
                     values=False):
                if finish:
                    weights(prev)
                if finish and not score:
                    combine_rest(prev)
                for b in range(NB):
                    if weigh and b == NB - 1:
                        p_low(cur, b)
                    if score:
                        add_mask(nxt, b)
                        if values and b == 0:
                            side_out(Tile(0, 1))
                            dve.wait_ge(s_gev, 1)
                            for c in range(DC):
                                nc.vector.tensor_scalar(xbar_bc[:, c], ones32[:, :], xbarT[:, c:c + 1], None, ALU.mult
                                                        ).then_inc(s_gev, 1)
                        if values and b == 1:
                            dve.wait_ge(s_gstep, 2)
                            dve.wait_ge(s_bc, 48)
                            nc.vector.tensor_tensor(gv_b[:, :], ps_pro[:, 0:D], bgv_b[:, :], ALU.add
                                                    ).then_inc(s_gev, 1)
                        if b == NB - 1:
                            row_max(nxt)
                    if b == 2 and finish and score:
                        combine_rest(prev)
                    if b == LAG and finish and score:
                        combine(prev)
                    if weigh and b < NB - 1:
                        p_low(cur, b)
                    if values and EARLY + b < NB:
                        for n in v_steps(EARLY + b):
                            v_low(n)
                    if b == 1 and project:
                        q_split(nxt2)
                        side_out(nxt2)
                if finish and not score:
                    combine(prev)

            schedule(dve, step)


def kernel(x, adj, L0_gnn_masked_x, L0_gnn_Wlq, L0_gnn_Wlk, L0_gnn_Wlv, L0_gnn_blv, L0_gnn_Wgq, L0_gnn_Wgk,
           L0_gnn_Wgv, L0_gnn_bgv, L0_gnn_Wes, L0_gnn_Wev, L0_gnn_bev):
    import numpy as np
    import concourse.bacc as bacc
    from concourse.bass_utils import run_bass_kernel_spmd as run

    mx = np.asarray(L0_gnn_masked_x)
    N, D = mx.shape
    arrays = {
        "x": np.asarray(x),
        "adj": np.asarray(adj),
        "mxT": mx.reshape(N // P, P, D // P, P).transpose(0, 3, 2, 1),
        "mx": mx,
        "WlqT": np.asarray(L0_gnn_Wlq).T,
        "WlkT": np.asarray(L0_gnn_Wlk).T,
        "Wlv": np.asarray(L0_gnn_Wlv),
        "blv": np.asarray(L0_gnn_blv),
        "WgqT": np.asarray(L0_gnn_Wgq).T,
        "WgkT": np.asarray(L0_gnn_Wgk).T,
        "Wgv": np.asarray(L0_gnn_Wgv),
        "bgv": np.asarray(L0_gnn_bgv),
        "Wes": np.asarray(L0_gnn_Wes),
        "Wev": np.asarray(L0_gnn_Wev),
        "bev": np.asarray(L0_gnn_bev),
    }
    arrays = {name: np.ascontiguousarray(a) for name, a in arrays.items()}
    nc = bacc.Bacc("TRN2", target_bir_lowering=False, num_devices=1)
    args = [nc.dram_tensor(name, a.shape, mybir.dt.from_np(a.dtype), kind="ExternalInput").ap()
            for name, a in arrays.items()]
    args.append(nc.dram_tensor("out", (N, D), F32, kind="ExternalOutput").ap())
    build(nc, *args)
    return run(nc, [arrays], core_ids=[0]).results[0]["out"]
```
